# Optimizing a Trainium2 kernel written in Bass

```python
import numpy as np
import jax
import jax.numpy as jnp

def _softmax(x, axis=-1):
    return jax.nn.softmax(x, axis=axis)

def _gelu(x):
    return jax.nn.gelu(x, approximate=True)

def _silu(x):
    return jax.nn.silu(x)

def _sigmoid(x):
    return jax.nn.sigmoid(x)

def _layernorm(x, axis=-1, eps=1e-05):
    m = jnp.mean(x, axis=axis, keepdims=True)
    v = jnp.var(x, axis=axis, keepdims=True)
    return (x - m) / jnp.sqrt(v + eps)

def _scatter_add(tgt, idx, src, axis=0):
    return tgt.at[idx].add(src)

def _segment_sum(src, seg, n):
    return jax.ops.segment_sum(src, seg, n)
kernel_name = 'mk_adaln_ffn_d2_seqx_r8_699d55'

def setup_inputs(seed: int=0):
    np.random.seed(seed)
    _w = jnp.asarray

    def _rec_inputs():
        import jax
        import jax.numpy as jnp
        _rk = jax.random.key(seed)
        x = -0.0003929 + 0.9999 * jax.random.normal(jax.random.fold_in(_rk, 1), (128, 32, 512), jnp.float32)
        _lenS = 32 - jax.random.randint(jax.random.fold_in(_rk, 7), (128,), 0, max(1, 32 // 4) + 1, jnp.int32)
        _lenS2 = 32 - jax.random.randint(jax.random.fold_in(_rk, 8), (128,), 0, max(1, 32 // 4) + 1, jnp.int32)
        itok_B_8_3872 = jax.random.randint(jax.random.fold_in(_rk, 11), (128,), 8, 3873, jnp.int32)
        itok_B_6_15 = jax.random.randint(jax.random.fold_in(_rk, 12), (128,), 6, 16, jnp.int32)
        return (x, itok_B_8_3872, itok_B_6_15)
    x, itok_B_8_3872, itok_B_6_15 = _rec_inputs()

    def _L0_cond_setup():
        import math
        import jax, jax.numpy as jnp
        import numpy as np
        H, N, B, L = (32, 64, 16, 512)
        DT_MIN, DT_MAX = (0.001, 0.1)

        def _get_kernel(log_dt, C, log_A_real, A_imag, length):
            Cc = C[..., 0] + 1j * C[..., 1]
            dt = jnp.exp(log_dt)
            A = -jnp.exp(log_A_real) + 1j * A_imag
            dtA = A * dt[:, None]
            P = dtA[:, :, None] * jnp.arange(length, dtype=jnp.float32)
            Cs = Cc * (jnp.exp(dtA) - 1.0) / A
            K = 2.0 * jnp.einsum('hn,hnl->hl', Cs, jnp.exp(P)).real
            return K
        key = jax.random.key(seed)
        ks = jax.random.split(key, 6)
        u = jax.random.normal(ks[0], (B, H, L), dtype=jnp.float32)
        length = jax.random.randint(ks[1], (B,), 0, L)
        log_dt = jax.random.uniform(ks[2], (H,), dtype=jnp.float32) * (math.log(DT_MAX) - math.log(DT_MIN)) + math.log(DT_MIN)
        C = jax.random.normal(ks[3], (H, N, 2), dtype=jnp.float32)
        log_A_real = jnp.log(0.5 * jnp.ones((H, N), dtype=jnp.float32))
        A_imag = math.pi * jnp.broadcast_to(jnp.arange(N, dtype=jnp.float32), (H, N))
        D = jax.random.normal(ks[4], (H,), dtype=jnp.float32)
        return {'u': u, 'length': length, 'log_dt': log_dt, 'C': C, 'log_A_real': log_A_real, 'A_imag': A_imag, 'D': D}
    _L0_cond_all = _L0_cond_setup()
    _L0_cond_in = {k: v for k, v in _L0_cond_all.items() if k in ('log_dt', 'C', 'log_A_real', 'A_imag', 'D')}
    del _L0_cond_all

    def _L0_ffn_setup():
        import jax, jax.numpy as jnp
        import numpy as np
        B, S, D, O, E, R = (4, 256, 512, 512, 8, 16)
        SCALING = 32.0 / 16.0
        MAX_THRESHOLD = 0.125
        key = jax.random.key(seed)
        ks = jax.random.split(key, 8)
        return {'x': jax.random.normal(ks[0], (B, S, D), jnp.float32), 'W_base': jax.random.normal(ks[1], (O, D), jnp.float32) * (1.0 / np.sqrt(D)), 'b_base': jax.random.normal(ks[2], (O,), jnp.float32) * 0.02, 'W_gate': jax.random.normal(ks[3], (E, D), jnp.float32) * (1.0 / np.sqrt(D)), 'W_thr': jax.random.normal(ks[4], (D,), jnp.float32) * (1.0 / np.sqrt(D)), 'b_thr': jax.random.normal(ks[5], (1,), jnp.float32) * 0.02, 'A_w': jax.random.normal(ks[6], (E, R, D), jnp.float32) * (1.0 / np.sqrt(D)), 'B_w': jax.random.normal(ks[7], (E, O, R), jnp.float32) * (1.0 / np.sqrt(R))}
    _L0_ffn_all = _L0_ffn_setup()
    _L0_ffn_in = {k: v for k, v in _L0_ffn_all.items() if k in ('W_base', 'b_base', 'W_gate', 'W_thr', 'b_thr', 'A_w', 'B_w')}
    del _L0_ffn_all

    def _L1_cond_setup():
        import jax, jax.numpy as jnp
        import numpy as np
        B, S, D_IN, D_OUT = (4, 256, 512, 512)
        RANK, MAX_LORAS = (16, 32)
        key = jax.random.key(seed)
        ks = jax.random.split(key, 6)
        x = jax.random.normal(ks[0], (B, S, D_IN), dtype=jnp.float32)
        adapter_ids = jax.random.randint(ks[1], (B,), 0, MAX_LORAS)
        base_weight = jax.random.normal(ks[2], (D_OUT, D_IN), dtype=jnp.float32) * D_IN ** (-0.5)
        base_bias = jax.random.normal(ks[3], (D_OUT,), dtype=jnp.float32) * 0.01
        lora_A_w = jax.random.normal(ks[4], (MAX_LORAS, RANK, D_IN), dtype=jnp.float32) * D_IN ** (-0.5)
        lora_B_w = jax.random.normal(ks[5], (MAX_LORAS, D_OUT, RANK), dtype=jnp.float32) * RANK ** (-0.5)
        return {'x': x, 'adapter_ids': adapter_ids, 'base_weight': base_weight, 'base_bias': base_bias, 'lora_A_w': lora_A_w, 'lora_B_w': lora_B_w}
    _L1_cond_all = _L1_cond_setup()
    _L1_cond_in = {k: v for k, v in _L1_cond_all.items() if k in ('base_weight', 'base_bias', 'lora_A_w', 'lora_B_w')}
    del _L1_cond_all

    def _L1_ffn_setup():
        import jax, jax.numpy as jnp
        import numpy as np
        B, S, H, I, R = (4, 32, 512, 1792, 4)

        def _anemll_linear(x, w, su, sv):
            w_eff = w * (su @ sv)
            return jnp.einsum('bsh,oh->bso', x, w_eff)
        key = jax.random.key(seed)
        ks = jax.random.split(key, 10)
        sd = 0.02
        return {'x': jax.random.normal(ks[0], (B, S, H), dtype=jnp.float32), 'gate_w': jax.random.normal(ks[1], (I, H), dtype=jnp.float32) * sd, 'gate_su': jax.random.normal(ks[2], (I, R), dtype=jnp.float32) * 0.5, 'gate_sv': jax.random.normal(ks[3], (R, H), dtype=jnp.float32) * 0.5, 'up_w': jax.random.normal(ks[4], (I, H), dtype=jnp.float32) * sd, 'up_su': jax.random.normal(ks[5], (I, R), dtype=jnp.float32) * 0.5, 'up_sv': jax.random.normal(ks[6], (R, H), dtype=jnp.float32) * 0.5, 'down_w': jax.random.normal(ks[7], (H, I), dtype=jnp.float32) * sd, 'down_su': jax.random.normal(ks[8], (H, R), dtype=jnp.float32) * 0.5, 'down_sv': jax.random.normal(ks[9], (R, I), dtype=jnp.float32) * 0.5}
    _L1_ffn_all = _L1_ffn_setup()
    _L1_ffn_in = {k: v for k, v in _L1_ffn_all.items() if k in ('gate_w', 'gate_su', 'gate_sv', 'up_w', 'up_su', 'up_sv', 'down_w', 'down_su', 'down_sv')}
    del _L1_ffn_all
    return {'x': x, 'itok_B_8_3872': itok_B_8_3872, 'itok_B_6_15': itok_B_6_15, 'L0_cond_log_dt': _L0_cond_in['log_dt'], 'L0_cond_C': _L0_cond_in['C'], 'L0_cond_log_A_real': _L0_cond_in['log_A_real'], 'L0_cond_A_imag': _L0_cond_in['A_imag'], 'L0_cond_D': _L0_cond_in['D'], 'L0_ffn_W_base': _L0_ffn_in['W_base'], 'L0_ffn_b_base': _L0_ffn_in['b_base'], 'L0_ffn_W_gate': _L0_ffn_in['W_gate'], 'L0_ffn_W_thr': _L0_ffn_in['W_thr'], 'L0_ffn_b_thr': _L0_ffn_in['b_thr'], 'L0_ffn_A_w': _L0_ffn_in['A_w'], 'L0_ffn_B_w': _L0_ffn_in['B_w'], 'L1_cond_base_weight': _L1_cond_in['base_weight'], 'L1_cond_base_bias': _L1_cond_in['base_bias'], 'L1_cond_lora_A_w': _L1_cond_in['lora_A_w'], 'L1_cond_lora_B_w': _L1_cond_in['lora_B_w'], 'L1_ffn_gate_w': _L1_ffn_in['gate_w'], 'L1_ffn_gate_su': _L1_ffn_in['gate_su'], 'L1_ffn_gate_sv': _L1_ffn_in['gate_sv'], 'L1_ffn_up_w': _L1_ffn_in['up_w'], 'L1_ffn_up_su': _L1_ffn_in['up_su'], 'L1_ffn_up_sv': _L1_ffn_in['up_sv'], 'L1_ffn_down_w': _L1_ffn_in['down_w'], 'L1_ffn_down_su': _L1_ffn_in['down_su'], 'L1_ffn_down_sv': _L1_ffn_in['down_sv']}

def reference(x, itok_B_8_3872, itok_B_6_15, L0_cond_log_dt, L0_cond_C, L0_cond_log_A_real, L0_cond_A_imag, L0_cond_D, L0_ffn_W_base, L0_ffn_b_base, L0_ffn_W_gate, L0_ffn_W_thr, L0_ffn_b_thr, L0_ffn_A_w, L0_ffn_B_w, L1_cond_base_weight, L1_cond_base_bias, L1_cond_lora_A_w, L1_cond_lora_B_w, L1_ffn_gate_w, L1_ffn_gate_su, L1_ffn_gate_sv, L1_ffn_up_w, L1_ffn_up_su, L1_ffn_up_sv, L1_ffn_down_w, L1_ffn_down_su, L1_ffn_down_sv):
    import jax
    import jax.numpy as jnp

    def _L0_cond_ref(u, length, log_dt, C, log_A_real, A_imag, D):
        import math
        import jax, jax.numpy as jnp
        import numpy as np
        H, N, B, L = (32, 64, 16, 512)
        DT_MIN, DT_MAX = (0.001, 0.1)

        def _get_kernel(log_dt, C, log_A_real, A_imag, length):
            Cc = C[..., 0] + 1j * C[..., 1]
            dt = jnp.exp(log_dt)
            A = -jnp.exp(log_A_real) + 1j * A_imag
            dtA = A * dt[:, None]
            P = dtA[:, :, None] * jnp.arange(length, dtype=jnp.float32)
            Cs = Cc * (jnp.exp(dtA) - 1.0) / A
            K = 2.0 * jnp.einsum('hn,hnl->hl', Cs, jnp.exp(P)).real
            return K
        Bq, Hq, Lq = u.shape
        mask = (jnp.arange(Lq) < length[:, None]).astype(u.dtype)
        u_m = u * mask[:, None, :]
        kernel = _get_kernel(log_dt, C, log_A_real, A_imag, Lq)
        n = 2 * Lq
        k_f = jnp.fft.rfft(kernel, n=n)
        u_f = jnp.fft.rfft(u_m, n=n)
        y = jnp.fft.irfft(u_f * k_f, n=n)[..., :Lq]
        y = y + u_m * D[:, None]
        return y * mask[:, None, :]

    def _L0_ffn_ref(x, W_base, b_base, W_gate, W_thr, b_thr, A_w, B_w):
        import jax, jax.numpy as jnp
        import numpy as np
        B, S, D, O, E, R = (4, 256, 512, 512, 8, 16)
        SCALING = 32.0 / 16.0
        MAX_THRESHOLD = 0.125
        base = jnp.einsum('bsd,od->bso', x, W_base) + b_base
        xf = x.reshape(-1, D)
        gate = jax.nn.softmax(xf @ W_gate.T, axis=-1)
        thr = jax.nn.sigmoid(xf @ W_thr + b_thr[0]) * MAX_THRESHOLD
        adapted = gate - thr[:, None]
        selected = (adapted >= 0).astype(x.dtype)
        w = adapted * selected
        wsum = jnp.sum(w, axis=-1, keepdims=True)
        wsum = jnp.where(wsum == 0, jnp.ones_like(wsum), wsum)
        w = w / wsum
        h = jnp.einsum('nd,erd->ner', xf, A_w)
        moe = jnp.einsum('ner,ne,eor->no', h, w, B_w) * SCALING
        return base + moe.reshape(base.shape)

    def _L1_cond_ref(x, adapter_ids, base_weight, base_bias, lora_A_w, lora_B_w):
        import jax, jax.numpy as jnp
        import numpy as np
        B, S, D_IN, D_OUT = (4, 256, 512, 512)
        RANK, MAX_LORAS = (16, 32)
        result = jnp.einsum('bsd,od->bso', x, base_weight) + base_bias
        A = lora_A_w[adapter_ids]
        Bw = lora_B_w[adapter_ids]
        h = jnp.einsum('bsd,brd->bsr', x, A)
        lora_out = jnp.einsum('bsr,bor->bso', h, Bw)
        result = result + lora_out
        return result.astype(x.dtype)

    def _L1_ffn_ref(x, gate_w, gate_su, gate_sv, up_w, up_su, up_sv, down_w, down_su, down_sv):
        import jax, jax.numpy as jnp
        import numpy as np
        B, S, H, I, R = (4, 32, 512, 1792, 4)

        def _anemll_linear(x, w, su, sv):
            w_eff = w * (su @ sv)
            return jnp.einsum('bsh,oh->bso', x, w_eff)
        a = _anemll_linear(x, gate_w, gate_su, gate_sv)
        b = _anemll_linear(x, up_w, up_su, up_sv)
        d = jax.nn.silu(a) * b
        return _anemll_linear(d, down_w, down_su, down_sv)
    x = x + _L0_ffn_ref(_L0_cond_ref(x, itok_B_8_3872, L0_cond_log_dt, L0_cond_C, L0_cond_log_A_real, L0_cond_A_imag, L0_cond_D), L0_ffn_W_base, L0_ffn_b_base, L0_ffn_W_gate, L0_ffn_W_thr, L0_ffn_b_thr, L0_ffn_A_w, L0_ffn_B_w)
    x = x + _L1_ffn_ref(_L1_cond_ref(x, itok_B_6_15, L1_cond_base_weight, L1_cond_base_bias, L1_cond_lora_A_w, L1_cond_lora_B_w), L1_ffn_gate_w, L1_ffn_gate_su, L1_ffn_gate_sv, L1_ffn_up_w, L1_ffn_up_su, L1_ffn_up_sv, L1_ffn_down_w, L1_ffn_down_su, L1_ffn_down_sv)
    return x

_drawn_inputs = setup_inputs


def setup_inputs(seed=0):
    import zlib

    import numpy as np

    out = dict(_drawn_inputs(seed))
    spreads = {'L0_cond_log_A_real': (-0.6931471824645996, 0.2)}
    factors = {'L0_ffn_b_base': 8.0, 'L1_cond_base_bias': 200.0}
    for name, (base, spread) in spreads.items():
        noise = np.random.default_rng([zlib.crc32(name.encode()), seed]).standard_normal(out[name].shape)
        drawn = base * np.exp(spread * noise) if base else spread * noise
        out[name] = jnp.asarray(drawn.astype(out[name].dtype))
    for name, factor in factors.items():
        out[name] = (out[name] * factor).astype(out[name].dtype)
    return out
```

```python
from contextlib import ExitStack
import math

import concourse.bass as bass
from concourse import mybir

F32 = mybir.dt.float32
F32R = mybir.dt.float32r
I32 = mybir.dt.int32
U32 = mybir.dt.uint32
ALU = mybir.AluOpType
ACT = mybir.ActivationFunctionType
AX = mybir.AxisListType

P = 128
BATCH, SEQ, DIM = 128, 32, 512
KD = DIM // P
NSTATE = 64
KROW = 640
EXPERTS, RANK0 = 8, 16
AGW = EXPERTS * RANK0 + EXPERTS + 2
ADAPTERS, RANK1 = 32, 16
HID = 1792
CH = HID // P
LR = 4
GT = 512
NG = BATCH * SEQ // GT
UT = 256
LA, LC = 16, 32
NPH = LA + LA + LC + 2
NDEC = LA + LC
HQ = 8

LOG2E = 1.4426950408889634
MAGIC = 12582912.0
LN2_HI, LN2_LO = 0.693359375, -2.12194440e-4
TWO_PI_1 = round(2 * math.pi * 2**9) / 2**9
TWO_PI_2 = round((2 * math.pi - TWO_PI_1) * 2**21) / 2**21
TWO_PI_3 = 2 * math.pi - TWO_PI_1 - TWO_PI_2
PI_IN = 3.1415925
PASSES = ((0, 0), (0, 1), (1, 0))
H_BANK = ((3, 0), (1, 2))
Z_BANK = (((3, 1), (0, 2)), ((2, 2), (3, 2)))


def wait(eng, sem, value):
    if isinstance(value, int) and value <= 0:
        return
    eng.wait_ge(sem, value)


def build(nc, t):
    ctx = ExitStack()
    with ctx:
        def sem(name):
            return ctx.enter_context(nc.semaphore(name))

        def sb(name, shape, dt=F32, scope=ctx):
            return scope.enter_context(nc.sbuf_tensor(name, shape, dt))

        def ps(name, shape, scope):
            return scope.enter_context(nc.psum_tensor(name, shape, F32))

        gate_w = sb("gate_w", [P, KD, HID])
        up_w = sb("up_w", [P, KD, HID])
        down_w = sb("down_w", [P, CH, DIM])
        wstage = sb("wstage", [P, KD, DIM])
        ident = sb("ident", [P, P])

        sa = ExitStack()
        base_r = sb("base_r", [P, 2, KD, DIM], F32R, sa)
        ag_raw = sb("ag_raw", [P, KD, AGW], F32, sa)
        ag_r = sb("ag_r", [P, 2, KD, AGW], F32R, sa)
        moeb_raw = sb("moeb_raw", [P, DIM], F32, sa)
        moeb_r = sb("moeb_r", [P, 2, DIM], F32R, sa)
        mask = sb("mask", [P, DIM], F32, sa)
        bias0 = sb("bias0", [P, DIM], F32, sa)
        len_i = sb("len_i", [P, 1], I32, sa)
        len_f = sb("len_f", [P, 1], F32, sa)
        nbthr = sb("nbthr", [P, 2], F32, sa)
        xa = sb("xa", [P, 2, DIM], F32, sa)
        um = sb("um", [P, 2, DIM], F32, sa)
        ut_r = sb("ut_r", [P, 2, 2, KD, P], F32R, sa)
        small = sb("small", [P, 2, 64], F32, sa)
        hw = sb("hw", [P, P], F32, sa)
        hwt_r = sb("hwt_r", [P, 2, 2, P], F32R, sa)
        thin_raw = [sb(f"thin_raw{m}", [P, DIM], F32, sa) for m in range(3)]
        thin_r = [sb(f"thin_r{m}", [P, DIM], F32R, sa) for m in range(3)]
        wide_raw = sb("wide_raw", [P, HID], F32, sa)
        wide_r = [sb(f"wide_r{m}", [P, HID], F32R, sa) for m in range(2)]
        scale_sb = sb("scale_sb", [P, 2, DIM], F32, sa)
        dvec = sb("dvec", [P, SEQ], F32, sa)
        s4 = ExitStack()
        pack = sb("pack", [P, 6, SEQ], F32, s4)
        mult = sb("mult", [P, 3, NPH], F32, s4)
        e_in = sb("e_in", [P, 2, SEQ], F32, s4)
        e_t = sb("e_t", [P, 2, SEQ], F32, s4)
        e_k = sb("e_k", [P, 2, SEQ], F32, s4)
        e_r = sb("e_r", [P, 2, SEQ], F32, s4)
        e_h = sb("e_h", [P, 2, SEQ], F32, s4)
        e_p = sb("e_p", [P, 2, SEQ], I32, s4)
        e_out = sb("e_out", [P, 2, SEQ], F32, s4)
        em1 = sb("em1", [P, SEQ], F32, s4)
        rho = sb("rho", [P, SEQ], F32, s4)
        theta = sb("theta", [P, SEQ], F32, s4)
        theta_h = sb("theta_h", [P, SEQ], F32R, s4)
        theta_l = sb("theta_l", [P, SEQ], F32, s4)
        cw = sb("cw", [P, 12, SEQ], F32, s4)
        pfac = sb("pfac", [P, SEQ, LA], F32, s4)
        decay = sb("decay", [P, SEQ, NDEC], F32, s4)
        zeros = sb("zeros", [SEQ, 2, P], F32, s4)
        trig = sb("trig", [P, SEQ, NPH], F32, s4)
        ph_t, ph_h, ph_l = (gate_w[:, n, 0:2 * HQ * NPH].rearrange("p (s h n) -> p s h n", s=2, h=HQ)
                            for n in range(3))
        s4.close()
        toep = sb("toep", [P, 2, 2, DIM], F32R, sa)
        k_sb = trig[0:LA, :, 0:LC]
        k_r = toep[0:LA, :, :, :].rearrange("a s t (h c) -> a s (t h) c", c=LC)
        xr = sb("xr", [P, 2, DIM], F32, sa)
        ym = sb("ym", [P, DIM], F32, sa)
        yt_r = sb("yt_r", [P, 2, 2, KD, P], F32R, sa)
        x1t = sb("x1t", [P, 2, DIM], F32, sa)
        pa = ExitStack()
        ps_tu = ps("ps_tu", [P, KD, P], pa)
        ps_y = ps("ps_y", [P, DIM], pa)
        ps_ty = ps("ps_ty", [P, KD, P], pa)
        ps_s = ps("ps_s", [P, DIM], pa)
        ps_th = ps("ps_th", [P, DIM], pa)
        ps_w0 = ps("ps_w0", [P, DIM], pa)
        ps_b = [ps(f"ps_b{n}", [P, DIM], pa) for n in range(2)]
        ps_w = [ps_w0, ps_b[1]]
        ps_k = [ps_y, ps_b[0]]
        pa.close()
        sa.close()

        sB = ExitStack()
        proj_r = sb("proj_r", [P, 2, KD, DIM], F32R, sB)
        bias1 = sb("bias1", [P, KD], F32, sB)
        blockmask = sb("blockmask", [P, UT], F32, sB)
        idx_i = sb("idx_i", [P, 2 * NG], I32, sB)
        idx_f = sb("idx_f", [P, 2 * NG], F32, sB)
        idx_u = sb("idx_u", [P, 2 * NG], U32, sB)
        rowid = sb("rowid", [P, 1], F32, sB)
        a_raw = sb("a_raw", [P, DIM], F32, sB)
        b_raw = sb("b_raw", [P, DIM], F32, sB)
        at_r = sb("at_r", [P, 2, KD, P], F32R, sB)
        bg_r = sb("bg_r", [P, 2, DIM], F32R, sB)
        hm = sb("hm", [P, UT], F32, sB)
        hm_r = sb("hm_r", [P, 2, UT], F32R, sB)
        xt = sb("xt", [P, 2, DIM], F32, sB)
        xt_r = [sb(f"xt_r{n}", [P, 2, KD, UT], F32R, sB) for n in range(2)]
        z_r = sb("z_r", [P, 2, KD, GT], F32R, sB)
        gate_r = [sb(f"gate_r{n}", [P, 2, KD, P], F32R, sB) for n in range(2)]
        up_r = [sb(f"up_r{n}", [P, 2, KD, P], F32R, sB) for n in range(2)]
        down_r = [sb(f"down_r{n}", [P, 2, DIM], F32R, sB) for n in range(2)]
        silu = sb("silu", [P, GT], F32, sB)
        act32 = sb("act32", [P, GT], F32, sB)
        act_r = [sb(f"act_r{n}", [P, 2, GT], F32R, sB) for n in range(2)]
        res = sb("res", [P, GT // P, DIM], F32, sB)
        pB = ExitStack()
        acc = [ps(f"acc{n}", [P, DIM], pB) for n in range(GT // P)]
        bank = [ps(f"bank{n}", [P, GT], pB) for n in range(4)]
        pB.close()
        sB.close()

        s_par = sem("s4_params_in")
        s_cst = sem("constants_in")
        s_w0 = sem("block0_weights_in")
        s_w0b = sem("block0_small_weights_in")
        s_proj = sem("proj_weights_in")
        s_big = [sem(f"{n}_weights_in") for n in ("up", "down", "gate")]
        s_thin = [sem(f"thin_scales{m}_in") for m in range(3)]
        s_wide = [sem(f"wide_scales{m}_in") for m in range(3)]
        s_zero = sem("scales_zeroed")
        s_thi = sem("scales_high")
        s_tsp = sem("scales_split")
        s_wfull = sem("scale_tile_full")
        s_wfree = sem("scale_tile_read")
        s_wcopy = sem("scale_tile_copied")
        s_wmul = sem("scale_tile_applied")
        s_gmul = sem("gate_tile_applied")
        s_step = sem("s4_vector_step")
        s_th = sem("theta_parts")
        s_prod = sem("phase_products")
        s_red = sem("phases_reduced")
        s_sin = sem("sines")
        s_decp = sem("decay_exponents")
        s_dec = sem("decays")
        s_fac = sem("factors")
        s_k = sem("kernels_in_psum")
        s_kc = sem("kernels_copied")
        s_kh = sem("kernels_high")
        s_ks = sem("kernels_split")
        s_kz = sem("kernel_pad_zeroed")
        s_kout = sem("kernels_in_dram")
        s_whi = sem("block0_weights_high")
        s_wsp = sem("block0_weights_split")
        s_mask = sem("mask_made")
        x_in = [sem(f"x_in{n}") for n in range(2)]
        toep_in = [sem(f"toeplitz_in{n}") for n in range(2)]
        xr_in = [sem(f"x_residual_in{n}") for n in range(2)]
        x1_out = [sem(f"x1_out{n}") for n in range(2)]
        um_done = sem("x_masked")
        tu_done = sem("u_transposed")
        ut_hi = sem("u_high")
        ut_done = sem("u_split")
        conv_done = sem("conv_done")
        ym_done = sem("y_masked")
        ty_done = sem("y_transposed")
        yt_hi = sem("y_high")
        yt_done = sem("y_split")
        ag_done = sem("lora_and_gates_done")
        sh_done = sem("gate_logits_shifted")
        ex_done = sem("gate_exps_done")
        g_step = sem("gate_vector_step")
        w_done = sem("expert_weights")
        hw_done = sem("h_weighted")
        thw_done = sem("h_transposed")
        hwt_hi = sem("h_high")
        hwt_done = sem("h_split")
        base_done = sem("base_done")
        moe_done = sem("mixture_done")
        xb_done = sem("residual_and_bias")
        x1_done = sem("x1_made")
        xt_in = sem("x1_tile_in")
        res_in = sem("residual_in")
        out_made = sem("out_made")
        out_out = sem("out_stored")
        idx_ready = sem("row_indices")
        idx_step = sem("row_index_step")
        s_b1 = sem("block1_constants_in")
        a_in = sem("adapter_a_in")
        b_in = sem("adapter_b_in")
        proj_hi = sem("proj_high")
        proj_split = sem("proj_split")
        xt_hi = sem("x1_high")
        xt_split = sem("x1_split")
        at_hi = sem("adapter_a_high")
        at_split = sem("adapter_a_split")
        bg_hi = sem("adapter_b_high")
        bg_split = sem("adapter_b_split")
        hm_made = sem("lora_h_masked")
        hm_hi = sem("lora_h_high")
        hm_split = sem("lora_h_split")
        z_hi = sem("z_high")
        z_split = sem("z_split")
        gate_hi = sem("gate_chunk_high")
        gate_split = sem("gate_chunk_split")
        up_hi = sem("up_chunk_high")
        up_split = sem("up_chunk_split")
        down_hi = sem("down_chunk_high")
        down_split = sem("down_chunk_split")
        silu_done = sem("silu_done")
        mul_done = sem("hidden_made")
        act_hi = sem("hidden_high")
        act_split = sem("hidden_split")
        down_done = sem("down_done")
        full = [sem(f"bank{n}_full") for n in range(4)]

        x_d, out_d = t["x"], t["out"]
        x1_d = nc.dram_tensor("x1_scratch", (BATCH, SEQ, DIM), F32, kind="Internal").ap()
        k_d = nc.dram_tensor("kernel_scratch", (SEQ, 2, KROW), F32, kind="Internal").ap()
        x1_tok = x1_d.rearrange("b h d -> (b h) d")
        out_tok = out_d.rearrange("b h d -> (b h) d")

        GW = HID // KD
        up_tiles = [(1, k, q) for q in range(KD) for k in range(KD)]
        down_tiles = [(2, c, 0) for c in range(CH)]
        gate_tiles = [(0, k, q) for q in range(KD) for k in range(KD)]
        pool_tiles = up_tiles + down_tiles
        wide_of = {1: 0, 2: 1, 0: 0}
        order = {1: 0, 2: 1, 0: 2}

        def tile_ops(tile):
            m, a, q = tile
            if m == 2:
                return wide_r[wide_of[m]][:, a * P:(a + 1) * P], thin_r[m][:, :], down_w[:, a, :], DIM
            w = gate_w if m == 0 else up_w
            return (thin_r[m][:, a * P:(a + 1) * P], wide_r[wide_of[m]][:, q * GW:(q + 1) * GW],
                    w[:, a, q * GW:(q + 1) * GW], GW)

        def position(i, off):
            if isinstance(i, int):
                h = 2 * i + off
                return h, h % 2, h // 2
            return 2 * i + off, off % 2, i + off // 2

        def exists(h):
            return not isinstance(h, int) or 0 <= h < SEQ

        def phase_a(eng, turn):
            for h in range(-5, 2):
                turn(0, h)
            with eng.Fori(1, SEQ // 2 - 3) as i:
                turn(i, 0)
                turn(i, 1)
            for h in range(SEQ - 6, SEQ + 1):
                turn(0, h)

        def at_chunk(c):
            return (c, c % 2, c // 2) if isinstance(c, int) else c

        def pair(i, first):
            return 2 * i + first, first % 2, i + first // 2

        block = ctx.enter_context(nc.Block())

        @block.sync
        def _(sp):
            sp.dma_start(pack[:], t["s4_pack"]).then_inc(s_par, 16)
            sp.dma_start(mult[:], t["phase_table"]).then_inc(s_par, 16)
            sp.dma_start(dvec[0:1, :], t["d_row"]).then_inc(s_par, 16)
            sp.dma_start(ident[:], t["ident"]).then_inc(s_cst, 16)
            sp.dma_start(mask[:], t["iota"].partition_broadcast(P)).then_inc(s_cst, 16)
            sp.dma_start(len_i[:], t["lengths"]).then_inc(s_cst, 16)
            sp.dma_start(nbthr[:, 0:1], t["b_thr"].partition_broadcast(P)).then_inc(s_cst, 16)
            sp.dma_start(bias0[:], t["b_base"].partition_broadcast(P)).then_inc(s_cst, 16)

            sp.wait_ge(s_zero, 1)

            def scales(m):
                thin, wide = (t["scale_thin"], t["scale_wide"])
                for q in range(4):
                    sp.dma_start(thin_raw[m][32 * q:32 * q + LR, :], thin[m]).then_inc(s_thin[m], 16)
                if order[m]:
                    sp.wait_ge(s_tsp, order[m])
                for q in range(4):
                    sp.dma_start(wide_raw[32 * q:32 * q + LR, :], wide[m]).then_inc(s_wide[m], 16)

            scales(1)
            sp.dma_start(up_w[:], t["up_wt"].rearrange("(k p) i -> p k i", p=P)).then_inc(s_big[0], 16)

            def load_x(i, off):
                h, slot, k = position(i, off)
                if exists(h):
                    wait(sp, um_done, h - 1)
                    sp.dma_start(xa[:, slot, :], x_d[:, bass.ds(h, 1), :].rearrange("b a d -> b (a d)")
                                 ).then_inc(x_in[slot], 16)

            sp.dma_start(wstage[:], t["base_wt"].rearrange("(k p) n -> p k n", p=P)).then_inc(s_w0, 16)
            sp.dma_start(ag_raw[:], t["ag_wt"].rearrange("(k p) n -> p k n", p=P)).then_inc(s_w0b, 16)
            sp.dma_start(moeb_raw[:], t["moe_bt"]).then_inc(s_w0b, 16)
            sp.dma_start(down_w[:], t["down_wt"].rearrange("(c p) n -> p c n", p=P)).then_inc(s_big[1], 16)
            load_x(0, 0)
            load_x(0, 1)
            scales(2)
            sp.wait_ge(s_sin, SEQ // HQ)
            sp.dma_start(gate_w[:], t["gate_wt"].rearrange("(k p) i -> p k i", p=P)).then_inc(s_big[2], 16)
            scales(0)

            sp.wait_ge(s_kz, 1)
            sp.dma_start(k_d[:, :, 0:P - 1], zeros[:, :, 0:P - 1]).then_inc(s_kout, 16)
            sp.wait_ge(s_ks, 1)
            for part in range(2):
                dst = bass.AP(tensor=k_d.tensor, offset=part * KROW + P - 1,
                              ap=[[LC, LA], [2 * KROW, SEQ], [1, LC]])
                sp.dma_start(dst, k_r[:, part, :, :].bitcast(F32)).then_inc(s_kout, 16)
            sp.wait_ge(s_kout, 48)
            sp.wait_ge(s_wsp, 2)
            sp.dma_start(wstage[:], t["proj_wt"].rearrange("(k p) n -> p k n", p=P)).then_inc(s_proj, 16)

            def load_toep(i, off):
                h, slot, k = position(i, off)
                if exists(h):
                    wait(sp, conv_done, h - 1)
                    src = bass.AP(tensor=k_d.tensor, offset=h * (2 * KROW), ap=[[1, P], [KROW, 2], [1, DIM]])
                    sp.dma_start(toep[:, slot, :, :].bitcast(F32), src).then_inc(toep_in[slot], 16)

            def load_xr(i, off):
                h, slot, k = position(i, off)
                if exists(h):
                    wait(sp, x1_done, h - 1)
                    sp.dma_start(xr[:, slot, :], x_d[:, bass.ds(h, 1), :].rearrange("b a d -> b (a d)")
                                 ).then_inc(xr_in[slot], 16)

            def store_x1(i, off):
                h, slot, k = position(i, off)
                if exists(h):
                    sp.wait_ge(x1_done, h + 1)
                    sp.dma_start(x1_d[:, bass.ds(h, 1), :].rearrange("b a d -> b (a d)"), x1t[:, slot, :]
                                 ).then_inc(x1_out[slot], 16)

            def turn(i, off):
                load_toep(i, off + 3)
                if not (isinstance(i, int) and 2 * i + off + 5 < 2):
                    load_x(i, off + 5)
                load_xr(i, off + 1)
                store_x1(i, off - 1)

            phase_a(sp, turn)
            for slot in range(2):
                sp.wait_ge(x1_out[slot], 16 * (SEQ // 2))

            sp.dma_start(bias1[:], t["bias1_cols"]).then_inc(s_b1, 16)
            sp.dma_start(blockmask[:], t["blockmask"]).then_inc(s_b1, 16)
            sp.dma_start(idx_i[:], t["adapter_rows"]).then_inc(s_b1, 16)
            sp.dma_start(rowid[:], t["rank_rows"]).then_inc(s_b1, 16)

            def load_xt(g, u):
                s = 2 * g + u
                if u:
                    sp.wait_ge(full[1], 10 * g + 1)
                elif not isinstance(g, int) or g:
                    sp.wait_ge(full[1], 10 * g - 8)
                sp.dma_start(xt[:], x1_tok[bass.ds(s * UT, UT), :].rearrange("(t p) d -> p t d", p=P)
                             ).then_inc(xt_in, 16)

            def load_res(g):
                wait(sp, out_out, 16 * g)
                sp.dma_start(res[:], x1_tok[bass.ds(g * GT, GT), :].rearrange("(t p) d -> p t d", p=P)
                             ).then_inc(res_in, 16)

            def store_out(g):
                sp.wait_ge(out_made, g + 2)
                sp.dma_start(out_tok[bass.ds(g * GT, GT), :].rearrange("(t p) d -> p t d", p=P), res[:]
                             ).then_inc(out_out, 16)

            load_xt(0, 0)
            load_xt(0, 1)
            load_xt(1, 0)
            load_res(0)
            load_xt(1, 1)
            store_out(0)
            with sp.Fori(1, NG - 1) as g:
                load_xt(g + 1, 0)
                load_res(g)
                load_xt(g + 1, 1)
                store_out(g)
            load_res(NG - 1)
            store_out(NG - 1)
            sp.wait_ge(out_out, 16 * NG)

        @block.gpsimd
        def _(pool):
            for m in range(3):
                pool.memset(thin_raw[m][:], 0.0)
            pool.memset(wide_raw[:], 0.0).then_inc(s_zero, 1)
            pool.wait_ge(s_par, 48)
            pool.wait_ge(s_th, 1)

            def by_mult(row, n0, n1, hs):
                return mult[:, row, n0:n1].unsqueeze(1).to_broadcast([P, hs, n1 - n0])

            for q in range(SEQ // HQ):
                hs = slice(q * HQ, (q + 1) * HQ)
                if q >= 2:
                    pool.wait_ge(s_red, q - 1)
                hi = theta_h[:, hs].bitcast(F32).unsqueeze(2).to_broadcast([P, HQ, NPH])
                lo = theta_l[:, hs].unsqueeze(2).to_broadcast([P, HQ, NPH])
                pool.tensor_tensor(ph_h[:, q % 2], hi, by_mult(0, 0, NPH, HQ), ALU.mult)
                pool.tensor_tensor(ph_l[:, q % 2], lo, by_mult(0, 0, NPH, HQ), ALU.mult).then_inc(s_prod, 1)
                pool.wait_ge(s_prod, 2 * q + 1)
                pool.tensor_tensor(ph_l[:, q % 2], ph_l[:, q % 2], by_mult(2, 0, NPH, HQ), ALU.add
                                   ).then_inc(s_prod, 1)
            pool.tensor_tensor(decay[:, :, 0:LA], rho[:].unsqueeze(2).to_broadcast([P, SEQ, LA]),
                               by_mult(0, 0, LA, SEQ), ALU.mult)
            pool.tensor_tensor(decay[:, :, LA:NDEC], rho[:].unsqueeze(2).to_broadcast([P, SEQ, LC]),
                               by_mult(0, 2 * LA, 2 * LA + LC, SEQ), ALU.mult).then_inc(s_decp, 1)
            pool.memset(zeros[:], 0.0).then_inc(s_kz, 1)
            pool.wait_ge(s_cst, 80)
            pool.wait_ge(s_mask, 2)

            def mask_x(i, off):
                h, slot, k = position(i, off)
                if exists(h):
                    wait(pool, tu_done, h - 1)
                    pool.wait_ge(x_in[slot], 16 * (k + 1))
                    back = bass.AP(tensor=um[:].tensor, offset=slot * DIM + P - 1,
                                   ap=[[2 * DIM, P], [P, KD], [-1, P]])
                    pool.tensor_tensor(back, xa[:, slot, :].rearrange("p (j m) -> p j m", m=P),
                                       mask[:].rearrange("p (j m) -> p j m", m=P), ALU.mult).then_inc(um_done, 1)

            mask_x(0, 0)
            mask_x(0, 1)
            for n, tile in enumerate(pool_tiles):
                _, _, w, width = tile_ops(tile)
                pool.wait_ge(s_wcopy, n + 1)
                if tile[1:] == (0, 0):
                    pool.wait_ge(s_big[order[tile[0]]], 16)
                pool.tensor_tensor(w, w, scale_sb[:, n % 2, 0:width], ALU.mult).then_inc(s_wmul, 1)

            def add_bias(i, off):
                h, slot, k = position(i, off)
                if exists(h):
                    pool.wait_ge(xr_in[slot], 16 * (k + 1))
                    pool.tensor_tensor(xr[:, slot, :], xr[:, slot, :], bias0[:], ALU.add).then_inc(xb_done, 1)

            def turn(i, off):
                if not (isinstance(i, int) and 2 * i + off + 4 < 2):
                    mask_x(i, off + 4)
                add_bias(i, off)

            phase_a(pool, turn)

            pool.wait_ge(idx_ready, 1)

            for s in range(2 * NG):
                g, u = divmod(s, 2)
                row = bass.IndirectOffsetOnAxis(ap=idx_u[:, s:s + 1], axis=0)
                if s:
                    pool.wait_ge(full[2], 10 * g + 1 if u else 10 * g - 8)
                pool.indirect_dma_start(a_raw[:], None, t["lora_a"], row).then_inc(a_in, 16)
                wait(pool, bg_split, s)
                pool.indirect_dma_start(b_raw[:], None, t["lora_b"], row).then_inc(b_in, 16)

        @block.scalar
        def _(act):
            def high(out, in_):
                return act.activation(out, in_, ACT.Copy)

            def high_scales(m):
                act.wait_ge(s_thin[m], 64)
                act.wait_ge(s_wide[m], 64)
                high(thin_r[m][:], thin_raw[m][:])
                high(wide_r[wide_of[m]][:], wide_raw[:]).then_inc(s_thi, 1)

            high_scales(1)

            for q in range(SEQ // HQ):
                act.wait_ge(s_red, q + 1)
                act.activation(trig[:, q * HQ:(q + 1) * HQ, :], ph_t[:, q % 2], ACT.Sin).then_inc(s_sin, 1)
            act.wait_ge(s_decp, 1)
            act.activation(decay[:], decay[:], ACT.Exp).then_inc(s_dec, 1)
            high_scales(2)

            act.wait_ge(s_w0, 16)
            high(base_r[:, 0], wstage[:]).then_inc(s_whi, 1)
            act.wait_ge(s_w0b, 32)
            high(ag_r[:, 0], ag_raw[:])
            high(moeb_r[:, 0], moeb_raw[:]).then_inc(s_whi, 1)

            def copy_scales(n):
                _, _, _, width = tile_ops(pool_tiles[n])
                act.wait_ge(s_wfull, n + 1)
                wait(act, s_wmul, n - 1)
                act.activation(scale_sb[:, n % 2, 0:width], ps_w[n % 2][:, 0:width], ACT.Copy
                               ).then_inc(s_wcopy, 1)

            KAT = len(pool_tiles)
            for n in range(KAT):
                copy_scales(n)
            act.wait_ge(s_kc, 3)
            high(k_r[:, 0], k_sb).then_inc(s_kh, 1)

            def u_high(i, off):
                h, slot, k = position(i, off)
                if exists(h):
                    act.wait_ge(tu_done, h + 1)
                    wait(act, conv_done, h - 1)
                    high(ut_r[:, slot, 0], ps_tu[:]).then_inc(ut_hi, 1)

            u_high(0, 0)
            act.wait_ge(s_wfull, len(up_tiles))
            high_scales(0)
            u_high(0, 1)

            def turn(i, off):
                h, slot, _ = position(i, off)
                p, pslot, _ = position(i, off - 1)
                if exists(p):
                    act.wait_ge(thw_done, p + 1)
                    wait(act, moe_done, p - 1)
                    high(hwt_r[:, pslot, 0], ps_th[:, 0:P]).then_inc(hwt_hi, 1)
                if exists(h):
                    sm = small[:, slot]
                    act.wait_ge(sh_done, h + 1)
                    act.activation(sm[:, 16:24], sm[:, 8:16], ACT.Exp, accum_out=sm[:, 1:2])
                    act.activation(sm[:, 2:3], ps_s[:, EXPERTS * RANK0 + EXPERTS:EXPERTS * RANK0 + EXPERTS + 1],
                                   ACT.Exp, bias=nbthr[:, 1:2], scale=-1.0).then_inc(ex_done, 1)
                n, nslot, _ = position(i, off + 1)
                if exists(n):
                    act.wait_ge(ty_done, n + 1)
                    wait(act, base_done, n - 1)
                    high(yt_r[:, nslot, 0], ps_ty[:]).then_inc(yt_hi, 1)
                if not (isinstance(i, int) and 2 * i + off + 3 < 2):
                    u_high(i, off + 3)

            phase_a(act, turn)

            act.wait_ge(s_proj, 16)
            act.wait_ge(x1_out[0], 16 * (SEQ // 2))
            act.wait_ge(x1_out[1], 16 * (SEQ // 2))
            high(proj_r[:, 0], wstage[:]).then_inc(proj_hi, 1)

            def split_gu(c):
                c, slot, _ = at_chunk(c)
                high(gate_r[slot][:, 0], gate_w[:, :, bass.ds(c * P, P)]).then_inc(gate_hi, 1)
                high(up_r[slot][:, 0], up_w[:, :, bass.ds(c * P, P)]).then_inc(up_hi, 1)

            def unit_in(g, u):
                for j in range(2):
                    act.wait_ge(full[j], 10 * g + u + 1)
                    high(xt_r[u][:, 0, 2 * j:2 * j + 2, :], bank[j][:].rearrange("p (k n) -> p k n", k=2)
                         ).then_inc(xt_hi, 1)
                act.wait_ge(full[2], 10 * g + u + 1)
                high(at_r[:, 0], bank[2][:].rearrange("p (k n) -> p k n", k=KD)).then_inc(at_hi, 1)

            def unit_b(g, u):
                act.wait_ge(b_in, 16 * (2 * g + u + 1))
                high(bg_r[:, 0], b_raw[:]).then_inc(bg_hi, 1)

            def unit_h(g, u):
                act.wait_ge(hm_made, 2 * g + u + 1)
                high(hm_r[:, 0], hm[:]).then_inc(hm_hi, 1)

            def unit_z(g, u, j):
                b, n = Z_BANK[u][j]
                act.wait_ge(full[b], 10 * g + n + 1)
                for o in range(2):
                    k = 2 * j + o
                    last = act.activation(z_r[:, 0, k, u * UT:(u + 1) * UT], bank[b][:, o * UT:(o + 1) * UT],
                                          ACT.Identity, bias=bias1[:, k:k + 1])
                last.then_inc(z_hi, 1)

            def chunk(g, c, nxt, mid=None):
                cc, slot, k = at_chunk(c)
                n = CH * g + cc
                act.wait_ge(down_done, n + 1)
                high(down_r[slot][:, 0], down_w[:, bass.ds(cc, 1), :].rearrange("p a d -> p (a d)")
                     ).then_inc(down_hi, 1)
                act.wait_ge(full[2 * slot], 10 * g + 4 + k)
                act.wait_ge(mul_done, n + 1)
                act.activation(silu[:], bank[2 * slot][:], ACT.Silu).then_inc(silu_done, 1)
                if mid:
                    mid()
                act.wait_ge(mul_done, n + 2)
                high(act_r[slot][:, 0], act32[:]).then_inc(act_hi, 1)
                if nxt is not None:
                    split_gu(nxt)

            def group(g, last):
                with act.Fori(0, CH // 2 - 1) as i:
                    chunk(g, pair(i, 0), pair(i, 2))
                    chunk(g, pair(i, 1), pair(i, 3))
                if last:
                    chunk(g, CH - 2, None)
                    chunk(g, CH - 1, None)
                    return
                chunk(g, CH - 2, 0)
                chunk(g, CH - 1, 1, mid=lambda: unit_in(g + 1, 0))
                unit_rest(g + 1)

            def unit_rest(g):
                unit_b(g, 0)
                unit_h(g, 0)
                unit_in(g, 1)
                unit_z(g, 0, 0)
                unit_z(g, 0, 1)
                unit_b(g, 1)
                unit_h(g, 1)
                unit_z(g, 1, 0)
                unit_z(g, 1, 1)

            act.wait_ge(s_b1, 64)
            split_gu(0)
            split_gu(1)
            unit_in(0, 0)
            unit_rest(0)
            with act.Fori(0, NG - 1) as g:
                group(g, False)
            group(NG - 1, True)

        @block.vector
        def _(dve):
            def low(out, whole, high_):
                return dve.tensor_tensor(out, whole, high_.bitcast(F32), ALU.subtract)

            dve.sem_inc(mul_done, 1)
            dve.sem_inc(act_split, 1)
            dve.sem_inc(out_made, 1)

            steps = [0]

            def step(ins):
                steps[0] += 1
                ins.then_inc(s_step, 1)
                dve.wait_ge(s_step, steps[0])

            def expm1(n, x):
                T, K, R, H, PW = (v[:, 0:n] for v in (e_t, e_k, e_r, e_h, e_p))
                step(dve.tensor_scalar(e_in[:, 0:n], x, -87.0, 88.0, ALU.max, ALU.min))
                x = e_in[:, 0:n]
                step(dve.tensor_scalar(T, x, LOG2E, MAGIC + 127.0, ALU.mult, ALU.add))
                step(dve.tensor_scalar(K, T, -(MAGIC + 127.0), None, ALU.add))
                step(dve.tensor_single_scalar(PW, T.bitcast(I32), 23, op=ALU.logical_shift_left))
                step(dve.scalar_tensor_tensor(R, K, -LN2_HI, x, ALU.mult, ALU.add))
                step(dve.scalar_tensor_tensor(R, K, -LN2_LO, R, ALU.mult, ALU.add))
                step(dve.tensor_scalar(H, R, 1.0 / 5040, None, ALU.mult))
                for c in (1.0 / 720, 1.0 / 120, 1.0 / 24, 1.0 / 6, 0.5, 1.0):
                    step(dve.scalar_tensor_tensor(H, H, c, R, ALU.add, ALU.mult))

            dve.wait_ge(s_par, 48)
            expm1(2, pack[:, 0:2, :])
            pw = e_p[:].bitcast(F32)
            step(dve.tensor_tensor(e_out[:], pw, e_h[:], ALU.mult))
            step(dve.tensor_tensor(e_out[:], e_out[:], pw, ALU.add))
            ea, dt, ai = e_out[:, 0, :], e_out[:, 1, :], pack[:, 2, :]
            step(dve.tensor_tensor(theta[:], ai, dt, ALU.mult))
            step(dve.tensor_copy(theta_h[:], theta[:]))
            dve.tensor_tensor(theta_l[:], theta[:], theta_h[:].bitcast(F32), ALU.subtract)
            step(dve.scalar_tensor_tensor(rho[:], ea, -1.0, dt, ALU.mult, ALU.mult))
            dve.sem_inc(s_th, 1)
            for q in range(SEQ // HQ):
                hs = slice(q * HQ, (q + 1) * HQ)
                T = ph_t[:, q % 2]
                if q >= 2:
                    dve.wait_ge(s_sin, q - 1)
                step(dve.tensor_tensor(T, theta[:, hs].unsqueeze(2).to_broadcast([P, HQ, NPH]),
                                       mult[:, 0, :].unsqueeze(1).to_broadcast([P, HQ, NPH]), ALU.mult))
                step(dve.scalar_tensor_tensor(T, T, 1.0 / (2 * math.pi),
                                              mult[:, 1, :].unsqueeze(1).to_broadcast([P, HQ, NPH]),
                                              ALU.mult, ALU.add))
                step(dve.tensor_scalar(T, T, MAGIC, None, ALU.add))
                step(dve.tensor_scalar(T, T, -MAGIC, None, ALU.add))
                dve.wait_ge(s_prod, 2 * (q + 1))
                H, L = ph_h[:, q % 2], ph_l[:, q % 2]
                step(dve.scalar_tensor_tensor(H, T, -TWO_PI_1, H, ALU.mult, ALU.add))
                step(dve.scalar_tensor_tensor(H, T, -TWO_PI_2, H, ALU.mult, ALU.add))
                step(dve.tensor_tensor(H, H, L, ALU.add))
                step(dve.scalar_tensor_tensor(H, T, -TWO_PI_3, H, ALU.mult, ALU.add))
                dve.tensor_scalar(T, H, -PI_IN, PI_IN, ALU.max, ALU.min).then_inc(s_red, 1)

            def low_scales(m, n):
                dve.wait_ge(s_thi, n + 1)
                thin = (thin_r[m], thin_raw[m])
                wide = (wide_r[wide_of[m]], wide_raw)
                stat, mov = (wide, thin) if m == 2 else (thin, wide)
                dve.tensor_tensor(stat[0][64:128], stat[1][64:128], stat[0][64:128].bitcast(F32), ALU.subtract)
                dve.tensor_tensor(mov[0][32:64], mov[1][32:64], mov[0][32:64].bitcast(F32), ALU.subtract)
                dve.tensor_tensor(mov[0][96:128], mov[1][96:128], mov[0][96:128].bitcast(F32), ALU.subtract
                                  ).then_inc(s_tsp, 1)

            low_scales(1, 0)
            expm1(1, rho[:].unsqueeze(1))
            pw = e_p[:, 0, :].bitcast(F32)
            step(dve.tensor_tensor(em1[:], pw, e_h[:, 0, :], ALU.mult))
            step(dve.scalar_tensor_tensor(em1[:], pw, -1.0, em1[:], ALU.add, ALU.add))
            dve.wait_ge(s_sin, SEQ // HQ)
            W, ER, EI, NR, NI, INV, T0, T1, AL, BE, CR = (cw[:, n, :] for n in range(11))
            s1, sh = trig[:, :, NPH - 2], trig[:, :, NPH - 1]
            step(dve.scalar_tensor_tensor(W, sh, -2.0, sh, ALU.mult, ALU.mult))
            step(dve.scalar_tensor_tensor(ER, em1[:], 1.0, W, ALU.add, ALU.mult))
            step(dve.tensor_tensor(ER, ER, em1[:], ALU.add))
            step(dve.scalar_tensor_tensor(EI, em1[:], 1.0, s1, ALU.add, ALU.mult))
            step(dve.tensor_tensor(CR, pack[:, 3, :], pack[:, 5, :], ALU.mult))
            ci = pack[:, 4, :]
            step(dve.tensor_tensor(NR, CR, ER, ALU.mult))
            step(dve.tensor_tensor(T0, ci, EI, ALU.mult))
            step(dve.tensor_tensor(NR, NR, T0, ALU.subtract))
            step(dve.tensor_tensor(NI, CR, EI, ALU.mult))
            step(dve.tensor_tensor(T0, ci, ER, ALU.mult))
            step(dve.tensor_tensor(NI, NI, T0, ALU.add))
            step(dve.tensor_tensor(T0, ea, ea, ALU.mult))
            step(dve.tensor_tensor(T1, ai, ai, ALU.mult))
            step(dve.tensor_tensor(T0, T0, T1, ALU.add))
            step(dve.reciprocal(INV, T0))
            step(dve.tensor_tensor(T0, NI, ai, ALU.mult))
            step(dve.tensor_tensor(T1, NR, ea, ALU.mult))
            step(dve.tensor_tensor(T0, T0, T1, ALU.subtract))
            step(dve.scalar_tensor_tensor(AL, T0, 2.0, INV, ALU.mult, ALU.mult))
            step(dve.tensor_tensor(T0, NR, ai, ALU.mult))
            step(dve.tensor_tensor(T1, NI, ea, ALU.mult))
            step(dve.tensor_tensor(T0, T0, T1, ALU.add))
            step(dve.scalar_tensor_tensor(BE, T0, 2.0, INV, ALU.mult, ALU.mult))
            sn, cs, qs = trig[:, :, 0:LA], trig[:, :, LA:2 * LA], trig[:, :, 2 * LA:2 * LA + LC]
            step(dve.tensor_tensor(sn, sn, BE.unsqueeze(2).to_broadcast([P, SEQ, LA]), ALU.mult))
            step(dve.tensor_tensor(pfac[:], cs, AL.unsqueeze(2).to_broadcast([P, SEQ, LA]), ALU.mult))
            step(dve.tensor_tensor(pfac[:], pfac[:], sn, ALU.add))
            dve.wait_ge(s_dec, 1)
            dve.tensor_tensor(pfac[:], pfac[:], decay[:, :, 0:LA], ALU.mult)
            dve.tensor_tensor(decay[:, :, LA:NDEC], decay[:, :, LA:NDEC], qs, ALU.mult).then_inc(s_fac, 1)

            dve.wait_ge(s_cst, 80)
            step(dve.tensor_copy(len_f[:], len_i[:]))
            dve.tensor_scalar(mask[:], mask[:], len_f[:, 0:1], None, ALU.is_lt).then_inc(s_mask, 1)
            dve.tensor_scalar(nbthr[:, 1:2], nbthr[:, 0:1], -1.0, None, ALU.mult).then_inc(s_mask, 1)
            low_scales(2, 1)
            dve.wait_ge(s_whi, 1)
            low(base_r[:, 1], wstage[:], base_r[:, 0]).then_inc(s_wsp, 1)
            dve.wait_ge(s_whi, 2)
            low(ag_r[:, 1], ag_raw[:], ag_r[:, 0])
            low(moeb_r[:, 1], moeb_raw[:], moeb_r[:, 0]).then_inc(s_wsp, 1)

            for j in range(2):
                dve.wait_ge(s_k, j + 1)
                hs = slice(j * SEQ // 2, (j + 1) * SEQ // 2)
                dve.tensor_copy(k_sb[:, hs, :], ps_k[j][0:LA, :].rearrange("a (h c) -> a h c", c=LC)
                                ).then_inc(s_kc, 1)
            dve.wait_ge(s_kc, 2)
            first = trig[0:1, :, 0:1].rearrange("a h c -> a (h c)")
            dve.tensor_tensor(first, first, dvec[0:1, :], ALU.add).then_inc(s_kc, 1)
            dve.wait_ge(s_kh, 1)
            low(k_r[:, 1], k_sb, k_r[:, 0]).then_inc(s_ks, 1)

            def u_low(i, off):
                h, slot, k = position(i, off)
                if exists(h):
                    dve.wait_ge(ut_hi, h + 1)
                    low(ut_r[:, slot, 1], ps_tu[:], ut_r[:, slot, 0]).then_inc(ut_done, 1)

            u_low(0, 0)
            low_scales(0, 2)
            u_low(0, 1)
            dve.wait_ge(s_big[2], 16)
            for n, tile in enumerate(gate_tiles):
                _, _, w, width = tile_ops(tile)
                dve.wait_ge(s_wfull, len(pool_tiles) + n + 1)
                dve.tensor_tensor(w, w, ps_w[n % 2][:, 0:width], ALU.mult).then_inc(s_gmul, 1)

            GS = 8
            def turn(i, off):
                h, slot, k = position(i, off)
                p, pslot, pk = position(i, off - 1)
                if exists(p):
                    dve.wait_ge(hwt_hi, p + 1)
                    low(hwt_r[:, pslot, 1], ps_th[:, 0:P], hwt_r[:, pslot, 0]).then_inc(hwt_done, 1)
                if exists(h):
                    sm = small[:, slot]
                    e0 = EXPERTS * RANK0
                    done = [0]

                    def gstep(ins):
                        done[0] += 1
                        ins.then_inc(g_step, 1)
                        dve.wait_ge(g_step, GS * h + done[0])

                    dve.wait_ge(ag_done, h + 1)
                    gstep(dve.tensor_reduce(sm[:, 0:1], ps_s[:, e0:e0 + EXPERTS], AX.X, ALU.max))
                    dve.tensor_scalar(sm[:, 8:16], ps_s[:, e0:e0 + EXPERTS], sm[:, 0:1], None, ALU.subtract
                                      ).then_inc(sh_done, 1)
                    dve.wait_ge(ex_done, h + 1)
                    gstep(dve.tensor_scalar(sm[:, 2:3], sm[:, 2:3], 1.0, 8.0, ALU.add, ALU.mult))
                    gstep(dve.reciprocal(sm[:, 3:5], sm[:, 1:3]))
                    gstep(dve.tensor_scalar(sm[:, 24:32], sm[:, 16:24], sm[:, 3:4], sm[:, 4:5],
                                            ALU.mult, ALU.subtract))
                    gstep(dve.tensor_scalar(sm[:, 24:32], sm[:, 24:32], 0.0, None, ALU.max))
                    gstep(dve.tensor_reduce(sm[:, 5:6], sm[:, 24:32], AX.X, ALU.add))
                    gstep(dve.scalar_tensor_tensor(sm[:, 5:6], sm[:, 5:6], 0.0, sm[:, 5:6],
                                                   ALU.is_equal, ALU.add))
                    gstep(dve.reciprocal(sm[:, 6:7], sm[:, 5:6]))
                    assert done[0] == GS
                    dve.tensor_scalar(sm[:, 32:40], sm[:, 24:32], sm[:, 6:7], 2.0, ALU.mult, ALU.mult
                                      ).then_inc(w_done, 1)
                    dve.wait_ge(w_done, h + 1)
                    dve.tensor_tensor(hw[:].rearrange("p (e r) -> p e r", r=RANK0),
                                      ps_s[:, 0:e0].rearrange("p (e r) -> p e r", r=RANK0),
                                      sm[:, 32:40].unsqueeze(2).to_broadcast([P, EXPERTS, RANK0]), ALU.mult
                                      ).then_inc(hw_done, 1)
                if exists(p):
                    dve.wait_ge(moe_done, p + 1)
                    dve.wait_ge(xb_done, p + 1)
                    wait(dve, x1_out[pslot], 16 * pk)
                    dve.tensor_tensor(x1t[:, pslot, :], ps_b[pslot][:], xr[:, pslot, :], ALU.add
                                      ).then_inc(x1_done, 1)
                n, nslot, _ = position(i, off + 1)
                if exists(n):
                    dve.wait_ge(yt_hi, n + 1)
                    low(yt_r[:, nslot, 1], ps_ty[:], yt_r[:, nslot, 0]).then_inc(yt_done, 1)
                if not (isinstance(i, int) and 2 * i + off + 3 < 2):
                    u_low(i, off + 3)
                v, vslot, _ = position(i, off + 2)
                if exists(v):
                    dve.wait_ge(conv_done, v + 1)
                    wait(dve, ty_done, v)
                    dve.tensor_tensor(ym[:], ps_y[:], mask[:], ALU.mult).then_inc(ym_done, 1)

            phase_a(dve, turn)

            dve.wait_ge(proj_hi, 1)
            low(proj_r[:, 1], wstage[:], proj_r[:, 0]).then_inc(proj_split, 1)
            dve.wait_ge(s_b1, 64)
            dve.tensor_copy(idx_f[:], idx_i[:]).then_inc(idx_step, 1)
            dve.wait_ge(idx_step, 1)
            dve.tensor_scalar(idx_f[:], idx_f[:], 0.0, float(ADAPTERS - 1), ALU.max, ALU.min).then_inc(idx_step, 1)
            dve.wait_ge(idx_step, 2)
            dve.tensor_scalar(idx_f[:], idx_f[:], float(RANK1), rowid[:, 0:1], ALU.mult, ALU.add
                              ).then_inc(idx_step, 1)
            dve.wait_ge(idx_step, 3)
            dve.tensor_copy(idx_u[:], idx_f[:]).then_inc(idx_ready, 1)

            def split_gu(c, n):
                c, slot, _ = at_chunk(c)
                dve.wait_ge(gate_hi, n + 1)
                low(gate_r[slot][:, 1], gate_w[:, :, bass.ds(c * P, P)], gate_r[slot][:, 0]).then_inc(gate_split, 1)
                dve.wait_ge(up_hi, n + 1)
                low(up_r[slot][:, 1], up_w[:, :, bass.ds(c * P, P)], up_r[slot][:, 0]).then_inc(up_split, 1)

            def unit_in(g, u):
                s = 2 * g + u
                for j in range(2):
                    dve.wait_ge(xt_hi, 2 * s + j + 1)
                    low(xt_r[u][:, 1, 2 * j:2 * j + 2, :], bank[j][:].rearrange("p (k n) -> p k n", k=2),
                        xt_r[u][:, 0, 2 * j:2 * j + 2, :]).then_inc(xt_split, 1)
                dve.wait_ge(at_hi, s + 1)
                low(at_r[:, 1], bank[2][:].rearrange("p (k n) -> p k n", k=KD), at_r[:, 0]).then_inc(at_split, 1)

            def unit_b(g, u):
                s = 2 * g + u
                dve.wait_ge(bg_hi, s + 1)
                low(bg_r[:, 1], b_raw[:], bg_r[:, 0]).then_inc(bg_split, 1)

            def unit_h(g, u):
                b, n = H_BANK[u]
                dve.wait_ge(full[b], 10 * g + n + 1)
                dve.tensor_tensor(hm[:], bank[b][:, 0:UT], blockmask[:], ALU.mult).then_inc(hm_made, 1)
                dve.wait_ge(hm_hi, 2 * g + u + 1)
                low(hm_r[:, 1], hm[:], hm_r[:, 0]).then_inc(hm_split, 1)

            def unit_z(g, u, j):
                b, n = Z_BANK[u][j]
                dve.wait_ge(z_hi, 4 * g + 2 * u + j + 1)
                for o in range(2):
                    k = 2 * j + o
                    last = dve.scalar_tensor_tensor(z_r[:, 1, k, u * UT:(u + 1) * UT],
                                                    bank[b][:, o * UT:(o + 1) * UT], bias1[:, k:k + 1],
                                                    z_r[:, 0, k, u * UT:(u + 1) * UT].bitcast(F32),
                                                    ALU.add, ALU.subtract)
                last.then_inc(z_split, 1)

            def chunk(g, c, nxt, mid=None):
                cc, slot, k = at_chunk(c)
                n = CH * g + cc
                dve.wait_ge(down_hi, n + 1)
                low(down_r[slot][:, 1], down_w[:, bass.ds(cc, 1), :].rearrange("p a d -> p (a d)"),
                    down_r[slot][:, 0]).then_inc(down_split, 1)
                dve.wait_ge(silu_done, n + 1)
                dve.wait_ge(full[2 * slot + 1], 10 * g + 4 + k)
                dve.wait_ge(act_split, n + 1)
                dve.tensor_tensor(act32[:], silu[:], bank[2 * slot + 1][:], ALU.mult).then_inc(mul_done, 1)
                dve.wait_ge(act_hi, n + 1)
                low(act_r[slot][:, 1], act32[:], act_r[slot][:, 0]).then_inc(act_split, 1)
                if mid:
                    mid()
                if nxt is not None:
                    split_gu(nxt, n + 2)

            def evacuate(g):
                dve.wait_ge(down_done, CH * (g + 1) + 2)
                dve.wait_ge(res_in, 16 * (g + 1))
                for n in range(GT // P):
                    last = dve.tensor_tensor(res[:, n, :], acc[n][:], res[:, n, :], ALU.add)
                last.then_inc(out_made, 1)

            def unit_rest(g):
                unit_b(g, 0)
                unit_h(g, 0)
                unit_in(g, 1)
                unit_z(g, 0, 0)
                unit_z(g, 0, 1)
                unit_b(g, 1)
                unit_h(g, 1)
                unit_z(g, 1, 0)
                unit_z(g, 1, 1)

            def group(g, last):
                with dve.Fori(0, CH // 2 - 1) as i:
                    chunk(g, pair(i, 0), pair(i, 2))
                    chunk(g, pair(i, 1), pair(i, 3))
                if last:
                    chunk(g, CH - 2, None)
                    chunk(g, CH - 1, None)
                    evacuate(g)
                    return
                chunk(g, CH - 2, 0)
                chunk(g, CH - 1, 1, mid=lambda: unit_in(g + 1, 0))
                unit_rest(g + 1)
                evacuate(g)

            split_gu(0, 0)
            split_gu(1, 1)
            unit_in(0, 0)
            unit_rest(0)
            with dve.Fori(0, NG - 1) as g:
                group(g, False)
            group(NG - 1, True)

        @block.tensor
        def _(pe):
            pe.sem_inc(down_done, 2)

            def split3(out, w, x, start=True, stop=True):
                n, total = 0, len(w) * len(PASSES)
                for wk, xk in zip(w, x):
                    for a, b in PASSES:
                        last = pe.matmul(out, wk[a], xk[b], start=start and n == 0, stop=stop and n == total - 1)
                        n += 1
                return last

            def scale_tile(n, tile, ready):
                lhs, rhs, _, width = tile_ops(tile)
                pe.wait_ge(s_tsp, ready)
                pe.matmul(ps_w[n % 2][:, 0:width], lhs, rhs, start=True, stop=True).then_inc(s_wfull, 1)

            for n, tile in enumerate(pool_tiles):
                wait(pe, s_wcopy, n - 1)
                scale_tile(n, tile, order[tile[0]] + 1)
            pe.wait_ge(s_fac, 1)
            for h in range(SEQ):
                j, hh = divmod(h, SEQ // 2)
                last = pe.matmul(ps_k[j][0:LA, hh * LC:(hh + 1) * LC], pfac[:, h, :], decay[:, h, LA:NDEC],
                                 start=True, stop=True)
                if hh == SEQ // 2 - 1:
                    last.then_inc(s_k, 1)

            def turn_u(i, off):
                h, slot, k = position(i, off)
                if exists(h):
                    pe.wait_ge(um_done, h + 1)
                    wait(pe, ut_done, h)
                    for j in range(KD):
                        last = pe.transpose(ps_tu[:, j, :], um[:, slot, j * P:(j + 1) * P], ident[:])
                    last.then_inc(tu_done, 1)

            pe.wait_ge(s_cst, 80)
            turn_u(0, 0)
            turn_u(0, 1)
            pe.wait_ge(s_wcopy, len(pool_tiles))
            for n, tile in enumerate(gate_tiles):
                wait(pe, s_gmul, n - 1)
                scale_tile(n, tile, 3)
            pe.wait_ge(s_wsp, 2)

            def turn(i, off):
                h, slot, k = position(i, off)
                p, pslot, _ = position(i, off - 1)
                n, nslot, _ = position(i, off + 1)
                v, vslot, vk = position(i, off + 2)
                yt = [[yt_r[:, slot, part, j, :] for part in range(2)] for j in range(KD)]
                if exists(h):
                    pe.wait_ge(yt_done, h + 1)
                    wait(pe, hw_done, h)
                    split3(ps_s[:, 0:AGW], yt, [[ag_r[:, part, j, :] for part in range(2)] for j in range(KD)]
                           ).then_inc(ag_done, 1)
                    wait(pe, x1_done, h - 1)
                    if isinstance(h, int) and h < 2:
                        pe.wait_ge(s_gmul, len(gate_tiles))
                    base = [[base_r[:, part, j, :] for part in range(2)] for j in range(KD)]
                    split3(ps_b[slot][:], yt[0:2], base[0:2], stop=False)
                if exists(p):
                    pe.wait_ge(hwt_done, p + 1)
                    split3(ps_b[pslot][:], [[hwt_r[:, pslot, part, :] for part in range(2)]],
                           [[moeb_r[:, part, :] for part in range(2)]], start=False).then_inc(moe_done, 1)
                if exists(n):
                    pe.wait_ge(ym_done, n + 1)
                    wait(pe, yt_done, n)
                    for j in range(KD):
                        last = pe.transpose(ps_ty[:, j, :], ym[:, j * P:(j + 1) * P], ident[:])
                    last.then_inc(ty_done, 1)
                if exists(h):
                    split3(ps_b[slot][:], yt[2:4], base[2:4], start=False, stop=False).then_inc(base_done, 1)
                if not (isinstance(i, int) and 2 * i + off + 3 < 2):
                    turn_u(i, off + 3)
                if exists(v):
                    pe.wait_ge(ut_done, v + 1)
                    pe.wait_ge(toep_in[vslot], 16 * (vk + 1))
                    wait(pe, ym_done, v)
                    for j in range(KD):
                        last = split3(ps_y[:, j * P:DIM], [[ut_r[:, vslot, part, j, :] for part in range(2)]],
                                      [[toep[:, vslot, part, 0:DIM - j * P] for part in range(2)]],
                                      start=j == 0, stop=j == KD - 1)
                    last.then_inc(conv_done, 1)
                if exists(h):
                    pe.wait_ge(hw_done, h + 1)
                    wait(pe, hwt_done, h)
                    pe.transpose(ps_th[:, 0:P], hw[:], ident[:]).then_inc(thw_done, 1)

            phase_a(pe, turn)

            def unit_in(g, u):
                s = 2 * g + u
                pe.wait_ge(xt_in, 16 * (s + 1))
                for j in range(2):
                    if u:
                        pe.wait_ge(xt_split, 4 * g + 1 + j)
                    elif j == 0:
                        wait(pe, silu_done, CH * g - 1)
                    else:
                        wait(pe, mul_done, CH * g)
                    for kk in range(2):
                        k = 2 * j + kk
                        for tt in range(2):
                            last = pe.transpose(bank[j][:, kk * UT + tt * P:kk * UT + (tt + 1) * P],
                                                xt[:, tt, k * P:(k + 1) * P], ident[:])
                    last.then_inc(full[j], 1)
                pe.wait_ge(a_in, 16 * (s + 1))
                if u:
                    pe.wait_ge(at_split, 2 * g + 1)
                else:
                    wait(pe, silu_done, CH * g)
                for k in range(KD):
                    last = pe.transpose(bank[2][:, k * P:(k + 1) * P], a_raw[:, k * P:(k + 1) * P], ident[:])
                last.then_inc(full[2], 1)

            def unit_h(g, u):
                b, _ = H_BANK[u]
                pe.wait_ge(xt_split, 4 * g + 2 * u + 2)
                pe.wait_ge(at_split, 2 * g + u + 1)
                if not u:
                    wait(pe, mul_done, CH * g + 1)
                split3(bank[b][:, 0:UT], [[at_r[:, part, k, :] for part in range(2)] for k in range(KD)],
                       [[xt_r[u][:, part, k, :] for part in range(2)] for k in range(KD)]).then_inc(full[b], 1)

            def unit_z(g, u, j):
                b, _ = Z_BANK[u][j]
                if (u, j) == (0, 0):
                    pe.wait_ge(hm_made, 2 * g + 1)
                elif (u, j) == (0, 1):
                    pe.wait_ge(xt_split, 4 * g + 3)
                elif (u, j) == (1, 0):
                    pe.wait_ge(at_split, 2 * g + 2)
                else:
                    pe.wait_ge(z_split, 4 * g + 1)
                for o in range(2):
                    c = 2 * j + o
                    out = bank[b][:, o * UT:(o + 1) * UT]
                    split3(out, [[proj_r[:, part, k, c * P:(c + 1) * P] for part in range(2)] for k in range(KD)],
                           [[xt_r[u][:, part, k, :] for part in range(2)] for k in range(KD)], stop=False)
                    if j == 0 and o == 0:
                        pe.wait_ge(hm_split, 2 * g + u + 1)
                        pe.wait_ge(bg_split, 2 * g + u + 1)
                    last = split3(out, [[bg_r[:, part, c * P:(c + 1) * P] for part in range(2)]],
                                  [[hm_r[:, part, :] for part in range(2)]], start=False)
                last.then_inc(full[b], 1)

            def gate_up(g, c):
                cc, slot, _ = at_chunk(c)
                n = CH * g + cc
                z = [[z_r[:, part, k, :] for part in range(2)] for k in range(KD)]
                for w, split, b, before in ((gate_r, gate_split, 2 * slot, silu_done),
                                            (up_r, up_split, 2 * slot + 1, mul_done)):
                    pe.wait_ge(split, n + 1)
                    if isinstance(c, int) and c < 2:
                        pe.wait_ge(z_split, 4 * g + 4)
                        pe.wait_ge(hm_made, 2 * g + 2)
                    else:
                        pe.wait_ge(before, n - 1 if before is silu_done else n)
                    last = split3(bank[b][:], [[w[slot][:, part, k, :] for part in range(2)] for k in range(KD)], z)
                    last.then_inc(full[b], 1)

            def down(g, c):
                cc, slot, _ = at_chunk(c)
                n = CH * g + cc
                pe.wait_ge(down_split, n + 1)
                pe.wait_ge(act_split, n + 2)
                if isinstance(c, int) and c == 0:
                    pe.wait_ge(out_made, g + 1)
                for tt in range(GT // P):
                    last = split3(acc[tt][:], [[act_r[slot][:, part, tt * P:(tt + 1) * P] for part in range(2)]],
                                  [[down_r[slot][:, part, :] for part in range(2)]],
                                  start=isinstance(c, int) and c == 0, stop=isinstance(c, int) and c == CH - 1)
                last.then_inc(down_done, 1)

            def group(g, last):
                gate_up(g, 0)
                gate_up(g, 1)
                down(g, 0)
                gate_up(g, 2)
                down(g, 1)
                with pe.Fori(1, CH // 2 - 1) as i:
                    gate_up(g, pair(i, 1))
                    down(g, pair(i, 0))
                    gate_up(g, pair(i, 2))
                    down(g, pair(i, 1))
                gate_up(g, CH - 1)
                if last:
                    down(g, CH - 2)
                    down(g, CH - 1)
                    return
                unit_in(g + 1, 0)
                down(g, CH - 2)
                unit_rest(g + 1)
                down(g, CH - 1)

            def unit_rest(g):
                unit_h(g, 0)
                unit_in(g, 1)
                unit_z(g, 0, 0)
                unit_z(g, 0, 1)
                unit_h(g, 1)
                unit_z(g, 1, 0)
                unit_z(g, 1, 1)

            pe.wait_ge(proj_split, 1)
            unit_in(0, 0)
            unit_rest(0)
            with pe.Fori(0, NG - 1) as g:
                group(g, False)
            group(NG - 1, True)


def kernel(**inputs):
    import numpy as np
    import concourse.bacc as bacc
    from concourse.bass_utils import run_bass_kernel_spmd

    a = {k: np.asarray(v) for k, v in inputs.items()}

    def con(v):
        return np.ascontiguousarray(v)

    def both(v):
        return np.concatenate([v.T, v.T], axis=0)

    f = np.float32
    cr, ci = a["L0_cond_C"][..., 0].T, a["L0_cond_C"][..., 1].T
    sign = np.concatenate([np.ones((NSTATE, SEQ), f), -np.ones((NSTATE, SEQ), f)])
    pack = np.stack([
        both(a["L0_cond_log_A_real"]),
        np.broadcast_to(a["L0_cond_log_dt"][None, :], (P, SEQ)),
        both(a["L0_cond_A_imag"]),
        np.concatenate([cr, ci]),
        np.concatenate([ci, cr]),
        sign], axis=1)
    la, lc = [LC * n for n in range(LA)], list(range(LC))
    table = np.zeros((P, 3, NPH), f)
    table[:, 0, :] = np.array(la + la + lc + [1, 0.5], f)
    table[:, 1, LA:2 * LA] = 0.25
    table[:NSTATE, 1, 2 * LA:2 * LA + LC] = 0.25
    table[:, 2, LA:2 * LA] = math.pi / 2
    table[:NSTATE, 2, 2 * LA:2 * LA + LC] = math.pi / 2
    rows = np.arange(P) // RANK1
    data = {
        "x": a["x"],
        "s4_pack": con(pack),
        "phase_table": table,
        "d_row": con(a["L0_cond_D"][None, :]),
        "ident": np.eye(P, dtype=f),
        "iota": np.arange(DIM, dtype=f),
        "lengths": con(a["itok_B_8_3872"][:, None]),
        "b_thr": a["L0_ffn_b_thr"],
        "b_base": a["L0_ffn_b_base"],
        "base_wt": con(a["L0_ffn_W_base"].T),
        "ag_wt": con(np.concatenate([a["L0_ffn_A_w"].reshape(EXPERTS * RANK0, DIM).T, a["L0_ffn_W_gate"].T,
                                     a["L0_ffn_W_thr"][:, None], np.zeros((DIM, 1), f)], axis=1)),
        "moe_bt": con(a["L0_ffn_B_w"].transpose(0, 2, 1).reshape(EXPERTS * RANK0, DIM)),
        "up_wt": con(a["L1_ffn_up_w"].T),
        "gate_wt": con(a["L1_ffn_gate_w"].T),
        "down_wt": con(a["L1_ffn_down_w"].T),
        "proj_wt": con(a["L1_cond_base_weight"].T),
        "bias1_cols": con(a["L1_cond_base_bias"].reshape(KD, P).T),
        "lora_a": con(a["L1_cond_lora_A_w"].reshape(ADAPTERS * RANK1, DIM)),
        "lora_b": con(a["L1_cond_lora_B_w"].transpose(0, 2, 1).reshape(ADAPTERS * RANK1, DIM)),
        "blockmask": con((np.arange(UT)[None, :] // SEQ == rows[:, None]).astype(f)),
        "adapter_rows": con(np.repeat(a["itok_B_6_15"].reshape(2 * NG, P // RANK1), RANK1, axis=1).T),
        "rank_rows": (np.arange(P) % RANK1).astype(f)[:, None],
        "scale_thin0": a["L1_ffn_gate_sv"], "scale_wide0": con(a["L1_ffn_gate_su"].T),
        "scale_thin1": a["L1_ffn_up_sv"], "scale_wide1": con(a["L1_ffn_up_su"].T),
        "scale_thin2": con(a["L1_ffn_down_su"].T), "scale_wide2": a["L1_ffn_down_sv"],
    }
    nc = bacc.Bacc("TRN2", target_bir_lowering=False, num_devices=1)
    t, arrays = {}, {}
    for name, v in data.items():
        v = np.ascontiguousarray(v)
        arrays[f"in_{name}"] = v
        t[name] = nc.dram_tensor(f"in_{name}", v.shape, mybir.dt.from_np(v.dtype), kind="ExternalInput").ap()
    t["scale_thin"] = [t[f"scale_thin{m}"] for m in range(3)]
    t["scale_wide"] = [t[f"scale_wide{m}"] for m in range(3)]
    t["out"] = nc.dram_tensor("out_x", (BATCH, SEQ, DIM), F32, kind="ExternalOutput").ap()
    build(nc, t)
    r = run_bass_kernel_spmd(nc, [arrays], core_ids=[0])
    return r.results[0]["out_x"]
```

```python
from contextlib import ExitStack
import math

import concourse.bass as bass
from concourse import mybir

F32 = mybir.dt.float32
F32R = mybir.dt.float32r
I32 = mybir.dt.int32
U32 = mybir.dt.uint32
ALU = mybir.AluOpType
ACT = mybir.ActivationFunctionType
AX = mybir.AxisListType

P = 128
BATCH, SEQ, DIM = 128, 32, 512
KD = DIM // P
NSTATE = 64
KROW = 640
EXPERTS, RANK0 = 8, 16
AGW = EXPERTS * RANK0 + EXPERTS + 2
ADAPTERS, RANK1 = 32, 16
HID = 1792
CH = HID // P
LR = 4
GW = HID // KD
SC_MOV = (0, HID, 2 * HID)
SC_STAT = (2 * HID + DIM, 2 * HID + 2 * DIM, 2 * HID + 3 * DIM)
SC_ALL = 3 * HID + 3 * DIM
GT = 512
NG = BATCH * SEQ // GT
UT = 256
LA, LC = 16, 32
PH_S, PH_C, PH_Q, NPH = 0, LA + 2, 2 * LA + 2, 2 * LA + 2 + LC
NDEC = LA + LC
HQ = 16

LOG2E = 1.4426950408889634
MAGIC = 12582912.0
LN2_HI, LN2_LO = 0.693359375, -2.12194440e-4
TWO_PI_1 = round(2 * math.pi * 2**9) / 2**9
TWO_PI_2 = 2 * math.pi - TWO_PI_1
HALF_TURN = 0.5 - 2.0**-24
PASSES = ((0, 0), (0, 1), (1, 0))
H_BANK = ((3, 0), (1, 2))
Z_BANK = (((3, 1), (0, 2)), ((2, 2), (3, 2)))


def wait(eng, sem, value):
    if isinstance(value, int) and value <= 0:
        return
    eng.wait_ge(sem, value)


def build(nc, t):
    ctx = ExitStack()
    with ctx:
        def sem(name):
            return ctx.enter_context(nc.semaphore(name))

        def sb(name, shape, dt=F32, scope=ctx):
            return scope.enter_context(nc.sbuf_tensor(name, shape, dt))

        def ps(name, shape, scope):
            return scope.enter_context(nc.psum_tensor(name, shape, F32))

        gate_w = sb("gate_w", [P, KD, HID])
        up_w = sb("up_w", [P, KD, HID])
        down_w = sb("down_w", [P, CH, DIM])
        wstage = sb("wstage", [P, KD, DIM])
        ident = sb("ident", [P, P])
        bias1 = sb("bias1", [P, KD])
        blockmask = sb("blockmask", [P, UT])
        idx_i = sb("idx_i", [P, 2 * NG], I32)
        idx_f = sb("idx_f", [P, 2 * NG])
        idx_u = sb("idx_u", [P, 2 * NG], U32)
        rowid = sb("rowid", [P, 1])
        a_raw = sb("a_raw", [P, DIM])
        b_raw = sb("b_raw", [P, DIM])

        sa = ExitStack()
        base_r = sb("base_r", [P, 2, KD, DIM], F32R, sa)
        ag_raw = sb("ag_raw", [P, KD, AGW], F32, sa)
        ag_r = sb("ag_r", [P, KD, 2, AGW], F32R, sa)
        moeb_raw = sb("moeb_raw", [P, DIM], F32, sa)
        moeb_r = sb("moeb_r", [P, 2, DIM], F32R, sa)
        mask = sb("mask", [P, DIM], F32, sa)
        bias0 = sb("bias0", [P, DIM], F32, sa)
        len_i = sb("len_i", [P, 1], I32, sa)
        len_f = sb("len_f", [P, 1], F32, sa)
        nbthr = sb("nbthr", [P, 2], F32, sa)
        xa = sb("xa", [P, 2, DIM], F32, sa)
        um = sb("um", [P, 2, KD, P], F32, sa)
        ut_r = sb("ut_r", [P, 2, 2, KD, P], F32R, sa)
        small = sb("small", [P, 2, 64], F32, sa)
        hw = sb("hw", [P, P], F32, sa)
        hwt_r = sb("hwt_r", [P, 2, 2, P], F32R, sa)
        ag_sum = sb("ag_sum", [P, AGW], F32, sa)
        scales_r = sb("scales_r", [P, SC_ALL], F32R, sa)
        mask_t = sb("mask_t", [P, KD, P], F32, sa)
        len_row = sb("len_row", [P, P], I32, sa)
        len_rowf = sb("len_rowf", [P, P], F32, sa)
        place = sb("place", [P, KD], F32, sa)
        s4 = ExitStack()
        pack = sb("pack", [P, 6, SEQ], F32, s4)
        mult = sb("mult", [P, NPH], F32, s4)
        offs = sb("offs", [P, 5], F32, s4)
        e_in = sb("e_in", [P, 2, SEQ], F32, s4)
        e_t = sb("e_t", [P, 2, SEQ], F32, s4)
        e_k = sb("e_k", [P, 2, SEQ], F32, s4)
        e_r = sb("e_r", [P, 2, SEQ], F32, s4)
        e_h = sb("e_h", [P, 2, SEQ], F32, s4)
        e_p = sb("e_p", [P, 2, SEQ], I32, s4)
        e_out = sb("e_out", [P, 2, SEQ], F32, s4)
        dpad = sb("dpad", [1, SEQ * LC], F32, s4)
        em1 = sb("em1", [P, SEQ], F32, s4)
        rho = sb("rho", [P, SEQ], F32, s4)
        theta = sb("theta", [P, SEQ], F32, s4)
        theta_h = sb("theta_h", [P, SEQ], F32R, s4)
        turns = sb("turns", [P, SEQ], F32, s4)
        theta_l = sb("theta_l", [P, SEQ], F32, s4)
        cw = sb("cw", [P, 18, SEQ], F32, s4)
        pfac = sb("pfac", [P, SEQ, LA], F32, s4)
        decay = sb("decay", [P, SEQ, NDEC], F32, s4)
        zeros = sb("zeros", [SEQ, 2, P], F32, s4)
        trig = sb("trig", [P, SEQ, NPH], F32, s4)
        GR, GI, INV2 = (cw[:, n, :] for n in (15, 16, 17))
        gate_flat = gate_w[:].rearrange("p k i -> p (k i)")
        ph_t, ph_h, ph_l = (gate_flat[:, n * SEQ * NPH:(n + 1) * SEQ * NPH].rearrange("p (h n) -> p h n", n=NPH)
                            for n in range(3))
        k_r = gate_flat[0:LA, 0:2 * SEQ * LC].rearrange("a (s h c) -> a s h c", s=2, c=LC).bitcast(F32R)
        scales_raw = down_w[:].rearrange("p c n -> p (c n)")[:, 0:SC_ALL]
        s4.close()
        toep = sb("toep", [P, 2, 2, DIM], F32R, sa)
        xr = sb("xr", [P, 2, DIM], F32, sa)
        ym = sb("ym", [P, DIM], F32, sa)
        yt_r = sb("yt_r", [P, 2, 2, KD, P], F32R, sa)
        x1t = sb("x1t", [P, 2, DIM], F32, sa)
        pa = ExitStack()
        ps_y = ps("ps_y", [P, DIM], pa)
        ps_ty = ps("ps_ty", [P, KD, P], pa)
        ps_s = ps("ps_s", [P, DIM], pa)
        ps_th = ps("ps_th", [P, DIM], pa)
        ps_w = [ps(f"ps_w{n}", [P, DIM], pa) for n in range(2)]
        ps_b = [ps(f"ps_b{n}", [P, DIM], pa) for n in range(2)]
        ps_k = [ps_y, ps_b[0]]
        free_banks = (ps_y, ps_ty[:].rearrange("p k n -> p (k n)"))
        pa.close()
        sa.close()

        sB = ExitStack()
        proj_r = sb("proj_r", [P, 2, KD, DIM], F32R, sB)
        at_r = sb("at_r", [P, 2, KD, P], F32R, sB)
        bg_r = sb("bg_r", [P, 2, DIM], F32R, sB)
        hm = sb("hm", [P, UT], F32, sB)
        hm_r = sb("hm_r", [P, 2, 2, UT], F32R, sB)
        xt = sb("xt", [P, 2, DIM], F32, sB)
        xt_r = [sb(f"xt_r{n}", [P, 2, KD, UT], F32R, sB) for n in range(2)]
        z_r = sb("z_r", [P, 2, KD, GT], F32R, sB)
        gate_r = [sb(f"gate_r{n}", [P, 2, KD, P], F32R, sB) for n in range(2)]
        up_r = [sb(f"up_r{n}", [P, 2, KD, P], F32R, sB) for n in range(2)]
        down_r = [sb(f"down_r{n}", [P, 2, DIM], F32R, sB) for n in range(2)]
        silu = sb("silu", [P, GT], F32, sB)
        act32 = sb("act32", [P, GT], F32, sB)
        act_r = [sb(f"act_r{n}", [P, 2, GT], F32R, sB) for n in range(2)]
        res = sb("res", [P, GT // P, DIM], F32, sB)
        pB = ExitStack()
        acc = [ps(f"acc{n}", [P, DIM], pB) for n in range(GT // P)]
        bank = [ps(f"bank{n}", [P, GT], pB) for n in range(4)]
        pB.close()
        sB.close()

        s_par = sem("s4_params_in")
        s_cst = sem("constants_in")
        s_w0 = sem("block0_weights_in")
        s_w0b = sem("block0_small_weights_in")
        s_proj = sem("proj_weights_in")
        s_big = [sem(f"{n}_weights_in") for n in ("up", "down", "gate")]
        s_scl = sem("scales_in")
        s_zero = sem("scales_zeroed")
        s_thi = sem("scales_high")
        s_tsp = sem("scales_split")
        s_wfull = sem("scale_tile_full")
        s_wmul = sem("scale_tile_applied")
        s_step = sem("s4_vector_step")
        s_th = sem("theta_parts")
        s_prod = sem("phase_products")
        s_inv = sem("reciprocal_of_A")
        s_pstep = sem("s4_gpsimd_step")
        s_red = sem("phases_reduced")
        s_sin = sem("sines")
        s_decp = sem("decay_exponents")
        s_dec = sem("decays")
        s_fac = sem("factors")
        s_k = sem("kernels_in_psum")
        s_kh = sem("kernels_high")
        s_ks = sem("kernels_split")
        s_kz = sem("kernel_pad_zeroed")
        s_kout = sem("kernels_in_dram")
        s_whi = sem("block0_weights_high")
        s_wsp = sem("block0_weights_split")
        s_mask = sem("mask_made")
        s_g = sem("s4_coefficients")
        x_in = [sem(f"x_in{n}") for n in range(2)]
        toep_in = [sem(f"toeplitz_in{n}") for n in range(2)]
        xr_in = [sem(f"x_residual_in{n}") for n in range(2)]
        x1_out = [sem(f"x1_out{n}") for n in range(2)]
        um_done = sem("x_masked")
        ut_hi = sem("u_high")
        ut_done = sem("u_split")
        conv_done = sem("conv_done")
        ym_done = sem("y_masked")
        ty_done = sem("y_transposed")
        yt_hi = sem("y_high")
        yt_done = sem("y_split")
        ag_done = sem("lora_and_gates_done")
        ag_copied = sem("lora_and_gates_copied")
        sh_done = sem("gate_logits_shifted")
        ex_done = sem("gate_exps_done")
        g_step = sem("gate_vector_step")
        w_done = sem("expert_weights")
        hw_done = sem("h_weighted")
        thw_done = sem("h_transposed")
        hwt_hi = sem("h_high")
        hwt_done = sem("h_split")
        base_done = sem("base_done")
        moe_done = sem("mixture_done")
        xb_done = sem("residual_and_bias")
        x1_done = sem("x1_made")
        xt_first = sem("first_x1_tile_in")
        xt_in = sem("x1_tile_in")
        res_in = sem("residual_in")
        out_made = sem("out_made")
        out_out = sem("out_stored")
        idx_ready = sem("row_indices")
        idx_step = sem("row_index_step")
        s_b1 = sem("block1_constants_in")
        a_in = sem("adapter_a_in")
        b_in = sem("adapter_b_in")
        proj_hi = sem("proj_high")
        proj_split = sem("proj_split")
        xt_hi = sem("x1_high")
        xt_split = sem("x1_split")
        at_hi = sem("adapter_a_high")
        at_split = sem("adapter_a_split")
        bg_hi = sem("adapter_b_high")
        bg_split = sem("adapter_b_split")
        hm_made = sem("lora_h_masked")
        hm_hi = sem("lora_h_high")
        hm_split = sem("lora_h_split")
        z_hi = sem("z_high")
        z_split = sem("z_split")
        gate_hi = sem("gate_chunk_high")
        gate_split = sem("gate_chunk_split")
        up_hi = sem("up_chunk_high")
        up_split = sem("up_chunk_split")
        down_hi = sem("down_chunk_high")
        down_split = sem("down_chunk_split")
        silu_done = sem("silu_done")
        mul_done = sem("hidden_made")
        act_hi = sem("hidden_high")
        act_split = sem("hidden_split")
        down_done = sem("down_done")
        tile_done = sem("last_tiles_done")
        tile_made = sem("last_tiles_made")
        full = [sem(f"bank{n}_full") for n in range(4)]

        x_d, out_d = t["x"], t["out"]
        x_t = t["x_t"]
        x1_d = nc.dram_tensor("x1_scratch", (BATCH, SEQ, DIM), F32, kind="Internal").ap()
        k_d = nc.dram_tensor("kernel_scratch", (SEQ, 2, KROW), F32, kind="Internal").ap()
        x1_tok = x1_d.rearrange("b h d -> (b h) d")
        out_tok = out_d.rearrange("b h d -> (b h) d")

        def tile_ops(m, a, q):
            if m == 2:
                return (scales_r[:, SC_STAT[2] + a * P:SC_STAT[2] + (a + 1) * P],
                        scales_r[:, SC_MOV[2]:SC_MOV[2] + DIM], down_w[:, a, :], DIM)
            w = gate_w if m == 0 else up_w
            return (scales_r[:, SC_STAT[m] + a * P:SC_STAT[m] + (a + 1) * P],
                    scales_r[:, bass.ds(q * GW + SC_MOV[m], GW)], w[:, a, bass.ds(q * GW, GW)], GW)

        def position(i, off):
            if isinstance(i, int):
                h = 2 * i + off
                return h, h % 2, h // 2
            return 2 * i + off, off % 2, i + off // 2

        def exists(h):
            return not isinstance(h, int) or 0 <= h < SEQ

        DOWN_TURNS = 4

        def down_tile(c):
            return 2 * KD * KD + c, 2, c, 0

        def phase_a(eng, turn):
            for h in range(-5, 2):
                turn(0, h, [])
            for m, first, end in ((1, 1, 5), (0, 5, 9), (None, 9, SEQ // 2 - 3)):
                with eng.Fori(first, end) as i:
                    for off in range(2):
                        turn(i, off, [] if m is None else
                             [(4 * (i - 1) + 2 * off + j, m, 2 * off + j, i - first) for j in range(2)])
            for n, h in enumerate(range(SEQ - 6, SEQ + 1)):
                turn(0, h, [down_tile(2 * n + j) for j in range(2)] if n < DOWN_TURNS else [])

        def at_chunk(c):
            return (c, c % 2, c // 2) if isinstance(c, int) else c

        def unit_order(g, u):
            return (2, 0, 1) if isinstance(g, int) and (g, u) == (0, 0) else (0, 1, 2)

        B_HALVES = (slice(0, DIM // 2), slice(DIM // 2, DIM))

        def pair(i, first):
            return 2 * i + first, first % 2, i + first // 2

        block = ctx.enter_context(nc.Block())

        @block.sync
        def _(sp):
            sp.dma_start(pack[:], t["s4_pack"]).then_inc(s_par, 16)
            sp.dma_start(mult[:], t["phase_table"]).then_inc(s_par, 16)
            sp.dma_start(offs[:], t["phase_offsets"]).then_inc(s_par, 16)
            sp.dma_start(len_row[:], t["lengths_row"].partition_broadcast(P)).then_inc(s_cst, 16)
            sp.dma_start(place[:], t["place"]).then_inc(s_cst, 16)
            sp.dma_start(ident[:], t["ident"]).then_inc(s_cst, 16)
            sp.dma_start(dpad[:], t["d_row"]).then_inc(s_cst, 16)
            sp.dma_start(mask[:], t["iota"].partition_broadcast(P)).then_inc(s_cst, 16)
            sp.dma_start(len_i[:], t["lengths"]).then_inc(s_cst, 16)
            sp.dma_start(nbthr[:, 0:1], t["b_thr"].partition_broadcast(P)).then_inc(s_cst, 16)
            sp.dma_start(bias0[:], t["b_base"].partition_broadcast(P)).then_inc(s_cst, 16)

            def load_x(i, off):
                h, slot, k = position(i, off)
                if exists(h):
                    wait(sp, um_done, h - 1)
                    sp.dma_start(xa[:, slot, :], x_t[bass.ds(h, 1)].rearrange("a p n -> p (a n)")
                                 ).then_inc(x_in[slot], 16)

            sp.dma_start(wstage[:], t["base_wt"].rearrange("(k p) n -> p k n", p=P)).then_inc(s_w0, 16)
            sp.dma_start(ag_raw[:], t["ag_wt"].rearrange("(k p) n -> p k n", p=P)).then_inc(s_w0b, 16)
            sp.dma_start(moeb_raw[:], t["moe_bt"]).then_inc(s_w0b, 16)
            load_x(0, 0)
            load_x(0, 1)
            sp.wait_ge(s_zero, 2)
            for q in range(4):
                sp.dma_start(scales_raw[32 * q:32 * q + LR, :], t["scales"]).then_inc(s_scl, 16)

            sp.dma_start(bias1[:], t["bias1_cols"]).then_inc(s_b1, 16)
            sp.dma_start(blockmask[:], t["blockmask"]).then_inc(s_b1, 16)
            sp.dma_start(idx_i[:], t["adapter_rows"]).then_inc(s_b1, 16)
            sp.dma_start(rowid[:], t["rank_rows"]).then_inc(s_b1, 16)
            sp.wait_ge(s_kz, 1)
            sp.dma_start(k_d[:, :, 0:P - 1], zeros[:, :, 0:P - 1]).then_inc(s_kout, 16)

            def store_kernels(j):
                sp.wait_ge(s_ks, j + 1)
                for part in range(2):
                    dst = bass.AP(tensor=k_d.tensor, offset=j * (SEQ // 2) * 2 * KROW + part * KROW + P - 1,
                                  ap=[[LC, LA], [2 * KROW, SEQ // 2], [1, LC]])
                    sp.dma_start(dst, k_r[:, part, j * SEQ // 2:(j + 1) * SEQ // 2, :].bitcast(F32)
                                 ).then_inc(s_kout, 16)

            store_kernels(0)
            sp.wait_ge(s_kout, 48)

            def load_toep(i, off):
                h, slot, k = position(i, off)
                if exists(h):
                    wait(sp, conv_done, h - 1)
                    src = bass.AP(tensor=k_d.tensor, offset=h * (2 * KROW), ap=[[1, P], [KROW, 2], [1, DIM]])
                    sp.dma_start(toep[:, slot, :, :].bitcast(F32), src).then_inc(toep_in[slot], 16)

            def load_xr(i, off):
                h, slot, k = position(i, off)
                if exists(h):
                    wait(sp, x1_done, h - 1)
                    sp.dma_start(xr[:, slot, :], x_d[:, bass.ds(h, 1), :].rearrange("b a d -> b (a d)")
                                 ).then_inc(xr_in[slot], 16)

            def store_x1(i, off):
                h, slot, k = position(i, off)
                if exists(h):
                    sp.wait_ge(x1_done, h + 1)
                    sp.dma_start(x1_d[:, bass.ds(h, 1), :].rearrange("b a d -> b (a d)"), x1t[:, slot, :]
                                 ).then_inc(x1_out[slot], 16)

            def turn(i, off, _):
                if isinstance(i, int) and off == -2:
                    sp.wait_ge(s_k, 2)
                load_toep(i, off + 3)
                if isinstance(i, int) and off == -2:
                    store_kernels(1)
                    sp.wait_ge(s_kout, 80)
                if isinstance(i, int) and off == SEQ - 6:
                    sp.wait_ge(s_wsp, 2)
                    sp.dma_start(wstage[:], t["proj_wt"].rearrange("(k p) n -> p k n", p=P)).then_inc(s_proj, 16)
                if not (isinstance(i, int) and 2 * i + off + 6 < 2):
                    load_x(i, off + 6)
                load_xr(i, off + 1)
                if not (isinstance(i, int) and off >= SEQ - 1):
                    store_x1(i, off - 1)

            phase_a(sp, turn)

            per = P // SEQ
            sp.wait_ge(x1_out[0], 16 * (SEQ // 2 - 1))
            sp.wait_ge(x1_out[1], 16 * (SEQ // 2 - 1))
            sp.wait_ge(ym_done, SEQ)
            sp.wait_ge(xb_done, SEQ)
            sp.wait_ge(ex_done, SEQ)
            for k in range(per):
                src = x1_d[0:2 * per].rearrange("(t k) h d -> k h t d", k=per)
                sp.dma_start(xt[k * SEQ:(k + 1) * SEQ - 2, :, :], src[k, 0:SEQ - 2]).then_inc(xt_first, 16)
            for h in (SEQ - 2, SEQ - 1):
                sp.wait_ge(x1_done, h + 1)
                for tt in range(2):
                    rows = bass.AP(tensor=xt[:].tensor, offset=h * 2 * DIM + tt * DIM,
                                   ap=[[SEQ * 2 * DIM, per], [1, DIM]])
                    sp.dma_start(rows, x1t[tt * per:(tt + 1) * per, h % 2, :]).then_inc(xt_first, 16)
            store_x1(0, SEQ - 2)
            store_x1(0, SEQ - 1)
            for slot in range(2):
                sp.wait_ge(x1_out[slot], 16 * (SEQ // 2))

            def load_xt(g, u):
                s = 2 * g + u
                if u:
                    sp.wait_ge(full[1], 10 * g + 1)
                elif not isinstance(g, int) or g:
                    sp.wait_ge(full[1], 10 * g - 8)
                sp.dma_start(xt[:], x1_tok[bass.ds(s * UT, UT), :].rearrange("(t p) d -> p t d", p=P)
                             ).then_inc(xt_in, 16)

            def load_res(g):
                wait(sp, out_out, 16 * g)
                sp.dma_start(res[:], x1_tok[bass.ds(g * GT, GT), :].rearrange("(t p) d -> p t d", p=P)
                             ).then_inc(res_in, 16)

            def store_out(g):
                sp.wait_ge(out_made, g + 2)
                sp.dma_start(out_tok[bass.ds(g * GT, GT), :].rearrange("(t p) d -> p t d", p=P), res[:]
                             ).then_inc(out_out, 16)

            load_xt(0, 1)
            load_xt(1, 0)
            load_res(0)
            load_xt(1, 1)
            store_out(0)
            with sp.Fori(1, NG - 1) as g:
                load_xt(g + 1, 0)
                load_res(g)
                load_xt(g + 1, 1)
                store_out(g)
            load_res(NG - 1)
            for n in range(GT // P):
                sp.wait_ge(tile_made, n + 1)
                sp.dma_start(out_tok[(NG - 1) * GT + n * P:(NG - 1) * GT + (n + 1) * P, :], res[:, n, :]
                             ).then_inc(out_out, 16)
            sp.wait_ge(out_out, 16 * (NG - 1 + GT // P))

        @block.gpsimd
        def _(pool):
            pool.memset(scales_raw[:, 0:SC_STAT[0]], 0.0).then_inc(s_zero, 1)
            pool.wait_ge(s_par, 48)
            pool.wait_ge(s_th, 1)

            def times(v, n0, n1, h0=0, h1=SEQ):
                return (v[:, h0:h1].unsqueeze(2).to_broadcast([P, h1 - h0, n1 - n0]),
                        mult[:, n0:n1].unsqueeze(1).to_broadcast([P, h1 - h0, n1 - n0]), ALU.mult)

            for q in range(SEQ // HQ):
                h0, h1 = q * HQ, (q + 1) * HQ
                pool.tensor_tensor(ph_h[:, h0:h1], *times(theta_h[:].bitcast(F32), 0, NPH, h0, h1)).then_inc(s_prod, 1)
                pool.tensor_tensor(ph_l[:, h0:h1], *times(theta_l, 0, NPH, h0, h1)).then_inc(s_prod, 1)
            pool.tensor_tensor(decay[:, :, 0:LA], *times(rho, PH_S, PH_S + LA))
            pool.tensor_tensor(decay[:, :, LA:NDEC], *times(rho, PH_Q, NPH)).then_inc(s_decp, 1)

            psteps = [0]

            def pstep(ins):
                psteps[0] += 1
                ins.then_inc(s_pstep, 1)
                pool.wait_ge(s_pstep, psteps[0])

            pool.wait_ge(s_inv, 1)
            CR, CA, CB, CC, CD = (cw[:, n, :] for n in range(5))
            ci, ea, ai = pack[:, 4, :], e_out[:, 0, :], pack[:, 2, :]
            pool.tensor_tensor(CA, ci, ai, ALU.mult)
            pool.tensor_tensor(CD, ci, ea, ALU.mult)
            pstep(pool.tensor_tensor(CR, pack[:, 3, :], pack[:, 5, :], ALU.mult))
            pool.tensor_tensor(CB, CR, ea, ALU.mult)
            pstep(pool.tensor_tensor(CC, CR, ai, ALU.mult))
            pool.tensor_tensor(CA, CA, CB, ALU.subtract)
            pstep(pool.tensor_tensor(CC, CC, CD, ALU.add))
            pool.tensor_tensor(GR, CA, INV2, ALU.mult)
            pool.tensor_tensor(GI, CC, INV2, ALU.mult).then_inc(s_g, 1)
            pieces = []
            for m in (1, 0, 2):
                nm, ns = (DIM, HID) if m == 2 else (HID, DIM)
                pieces += [(SC_MOV[m], nm, 32, 64), (SC_MOV[m], nm, 96, 128), (SC_STAT[m], ns, 64, 128)]

            def low_scales(n, before, count):
                n0, width, p0, p1 = pieces[n]
                pool.wait_ge(s_thi, (1, 1, 3, 2, 2, 3, 3, 3, 3)[n])
                wait(pool, s_tsp, n)
                pool.wait_ge(before, count)
                whole = scales_raw[p0:p1, n0:n0 + width]
                part = scales_r[p0:p1, n0:n0 + width]
                pool.tensor_tensor(part, whole, part.bitcast(F32), ALU.subtract).then_inc(s_tsp, 1)
                pool.wait_ge(s_tsp, n + 1)

            low_scales(0, s_g, 1)
            pool.wait_ge(s_dec, 1)
            pool.wait_ge(s_sin, SEQ // HQ)
            pool.tensor_tensor(decay[:, :, LA:NDEC], decay[:, :, LA:NDEC], trig[:, :, PH_Q:NPH], ALU.mult
                               ).then_inc(s_fac, 1)
            pool.memset(zeros[:], 0.0).then_inc(s_kz, 1)
            low_scales(1, s_kz, 1)
            pool.wait_ge(s_mask, 1)

            def mask_x(i, off):
                h, slot, k = position(i, off)
                if exists(h):
                    wait(pool, ut_done, h - 1)
                    pool.wait_ge(x_in[slot], 16 * (k + 1))
                    pool.tensor_tensor(um[:, slot], xa[:, slot].rearrange("p (j b) -> p j b", b=P), mask_t[:],
                                       ALU.mult).then_inc(um_done, 1)

            mask_x(0, 0)
            mask_x(0, 1)
            pool.wait_ge(s_cst, 16 * 8)

            def add_bias(i, off):
                h, slot, k = position(i, off)
                if exists(h):
                    pool.wait_ge(xr_in[slot], 16 * (k + 1))
                    pool.tensor_tensor(xr[:, slot, :], xr[:, slot, :], bias0[:], ALU.add).then_inc(xb_done, 1)

            def turn(i, off, _):
                early = isinstance(i, int) and 2 * i + off < 2
                if not (early and 2 * i + off + 5 < 2):
                    mask_x(i, off + 5)
                if early:
                    for n in {-4: [2], -3: [3], -2: [4], -1: [5, 6], 0: [7], 1: [8]}.get(off, []):
                        low_scales(n, um_done, max(2, off + 6))
                add_bias(i, off)

            phase_a(pool, turn)

            pool.wait_ge(idx_ready, 1)

            for s in range(2 * NG):
                g, u = divmod(s, 2)
                row = bass.IndirectOffsetOnAxis(ap=idx_u[:, s:s + 1], axis=0)
                if s:
                    pool.wait_ge(full[2], 10 * g + 1 if u else 10 * g - 8)
                pool.indirect_dma_start(a_raw[:], None, t["lora_a"], row).then_inc(a_in, 16)
                wait(pool, bg_split, 2 * s)
                pool.indirect_dma_start(b_raw[:], None, t["lora_b"], row).then_inc(b_in, 16)

        @block.scalar
        def _(act):
            def high(out, in_):
                return act.activation(out, in_, ACT.Copy)

            act.wait_ge(s_par, 48)
            act.wait_ge(s_w0, 16)
            act.wait_ge(s_scl, 64)
            act.dma_start(up_w[:], t["up_wt"].rearrange("(k p) i -> p k i", p=P)).then_inc(s_big[1], 16)

            def high_scales(n):
                act.wait_ge(s_scl, 64)
                n0, n1 = ((SC_MOV[1], SC_MOV[2]), (SC_MOV[0], SC_MOV[1]), (SC_MOV[2], SC_ALL))[n]
                high(scales_r[:, n0:n1], scales_raw[:, n0:n1]).then_inc(s_thi, 1)

            for q in range(SEQ // HQ):
                act.wait_ge(s_red, q + 1)
                hs = slice(q * HQ, (q + 1) * HQ)
                for n0, n1, bias in ((PH_S, PH_C, 0.0), (PH_C, PH_Q, offs[:, 4:5]), (PH_Q, NPH, offs[:, 3:4])):
                    last = act.activation(trig[:, hs, n0:n1], ph_t[:, hs, n0:n1], ACT.Sin,
                                          bias=bias, scale=2 * math.pi)
                last.then_inc(s_sin, 1)
                if q == 0:
                    high_scales(0)
            act.wait_ge(s_decp, 1)
            act.activation(decay[:], decay[:], ACT.Exp).then_inc(s_dec, 1)
            high_scales(1)
            high_scales(2)

            for j in range(2):
                act.wait_ge(s_k, j + 1)
                high(k_r[:, 0, j * SEQ // 2:(j + 1) * SEQ // 2, :],
                     ps_k[j][0:LA, :].rearrange("a (h c) -> a h c", c=LC)).then_inc(s_kh, 1)

            def u_high(i, off):
                h, slot, k = position(i, off)
                if exists(h):
                    act.wait_ge(um_done, h + 1)
                    wait(act, conv_done, h - 1)
                    high(ut_r[:, slot, 0], um[:, slot]).then_inc(ut_hi, 1)

            u_high(0, 0)
            u_high(0, 1)
            act.wait_ge(s_w0, 16)
            high(base_r[:, 0], wstage[:]).then_inc(s_whi, 1)
            act.wait_ge(s_w0b, 32)
            high(ag_r[:, :, 0], ag_raw[:])
            high(moeb_r[:, 0], moeb_raw[:]).then_inc(s_whi, 1)

            def turn(i, off, tiles):
                h, slot, _ = position(i, off)
                p, pslot, _ = position(i, off - 1)
                if exists(p):
                    act.wait_ge(thw_done, p + 1)
                    wait(act, moe_done, p - 1)
                    high(hwt_r[:, pslot, 0], ps_th[:, 0:P]).then_inc(hwt_hi, 1)
                if not (isinstance(i, int) and 2 * i + off + 3 < 2):
                    u_high(i, off + 3)
                if exists(h):
                    act.wait_ge(ag_done, h + 1)
                    wait(act, hw_done, h)
                    act.activation(ag_sum[:], ps_s[:, AGW:2 * AGW], ACT.Copy).then_inc(ag_copied, 1)
                    sm = small[:, slot]
                    act.wait_ge(sh_done, h + 1)
                    act.activation(sm[:, 16:24], sm[:, 8:16], ACT.Exp, accum_out=sm[:, 1:2])
                    act.activation(sm[:, 2:3], ag_sum[:, EXPERTS * RANK0 + EXPERTS:EXPERTS * RANK0 + EXPERTS + 1],
                                   ACT.Exp, bias=nbthr[:, 1:2], scale=-1.0).then_inc(ex_done, 1)
                n, nslot, _ = position(i, off + 1)
                if exists(n):
                    act.wait_ge(ty_done, n + 1)
                    wait(act, base_done, n - 1)
                    high(yt_r[:, nslot, 0], ps_ty[:]).then_inc(yt_hi, 1)
                if tiles and off == 0 and tiles[0][1] == 1:
                    q = tiles[0][3]
                    act.wait_ge(s_kout, 80)
                    act.dma_start(gate_w[:, bass.ds(q, 1), :],
                                  t["gate_wt"].rearrange("(k p) i -> p k i", p=P)[:, bass.ds(q, 1), :]
                                  ).then_inc(s_big[0], 16)
                if tiles and off == 0 and tiles[0][1] == 0:
                    q = tiles[0][3]
                    act.wait_ge(s_tsp, 9)
                    act.dma_start(down_w[:, :, bass.ds(q * P, P)],
                                  t["down_wt"].rearrange("(c p) n -> p c n", p=P)[:, :, bass.ds(q * P, P)]
                                  ).then_inc(s_big[2], 16)

            phase_a(act, turn)

            act.wait_ge(s_proj, 16)
            act.wait_ge(base_done, SEQ)
            high(proj_r[:, 0], wstage[:]).then_inc(proj_hi, 1)

            def split_gu(c):
                c, slot, _ = at_chunk(c)
                high(gate_r[slot][:, 0], gate_w[:, :, bass.ds(c * P, P)]).then_inc(gate_hi, 1)
                high(up_r[slot][:, 0], up_w[:, :, bass.ds(c * P, P)]).then_inc(up_hi, 1)

            def unit_in(g, u):
                for j in unit_order(g, u):
                    act.wait_ge(full[j], 10 * g + u + 1)
                    if j == 2:
                        high(at_r[:, 0], bank[2][:].rearrange("p (k n) -> p k n", k=KD)).then_inc(at_hi, 1)
                    else:
                        high(xt_r[u][:, 0, 2 * j:2 * j + 2, :], bank[j][:].rearrange("p (k n) -> p k n", k=2)
                             ).then_inc(xt_hi, 1)

            def unit_b(g, u):
                if u:
                    b, n = Z_BANK[0][1]
                    act.wait_ge(full[b], 10 * g + n + 1)
                act.wait_ge(b_in, 16 * (2 * g + u + 1))
                for cols in B_HALVES:
                    high(bg_r[:, 0, cols], b_raw[:, cols]).then_inc(bg_hi, 1)

            def unit_h(g, u):
                act.wait_ge(hm_made, 2 * g + u + 1)
                high(hm_r[:, u, 0], hm[:]).then_inc(hm_hi, 1)

            def unit_z(g, u, j):
                b, n = Z_BANK[u][j]
                act.wait_ge(full[b], 10 * g + n + 1)
                for o in range(2):
                    k = 2 * j + o
                    last = act.activation(z_r[:, 0, k, u * UT:(u + 1) * UT], bank[b][:, o * UT:(o + 1) * UT],
                                          ACT.Identity, bias=bias1[:, k:k + 1])
                last.then_inc(z_hi, 1)

            def chunk(g, c, nxt, mid=None):
                cc, slot, k = at_chunk(c)
                n = CH * g + cc
                act.wait_ge(down_done, n + 1)
                high(down_r[slot][:, 0], down_w[:, bass.ds(cc, 1), :].rearrange("p a d -> p (a d)")
                     ).then_inc(down_hi, 1)
                act.wait_ge(full[2 * slot], 10 * g + 4 + k)
                act.wait_ge(mul_done, n + 1)
                act.activation(silu[:], bank[2 * slot][:], ACT.Silu).then_inc(silu_done, 1)
                if mid:
                    mid()
                act.wait_ge(mul_done, n + 2)
                high(act_r[slot][:, 0], act32[:]).then_inc(act_hi, 1)
                if nxt is not None:
                    split_gu(nxt)

            def group(g, last):
                with act.Fori(0, CH // 2 - 1) as i:
                    chunk(g, pair(i, 0), pair(i, 2))
                    chunk(g, pair(i, 1), pair(i, 3))
                if last:
                    chunk(g, CH - 2, None)
                    chunk(g, CH - 1, None)
                    return
                chunk(g, CH - 2, 0)
                chunk(g, CH - 1, 1, mid=lambda: unit_in(g + 1, 0))
                unit_rest(g + 1)

            def unit_rest(g, mid=None):
                unit_b(g, 0)
                unit_h(g, 0)
                unit_in(g, 1)
                if mid:
                    mid()
                unit_z(g, 0, 0)
                unit_h(g, 1)
                unit_b(g, 1)
                unit_z(g, 0, 1)
                unit_z(g, 1, 0)
                unit_z(g, 1, 1)

            act.wait_ge(s_b1, 64)
            unit_in(0, 0)
            unit_rest(0, lambda: (split_gu(0), split_gu(1)))
            with act.Fori(0, NG - 1) as g:
                group(g, False)
            group(NG - 1, True)

        @block.vector
        def _(dve):
            def low(out, whole, high_):
                return dve.tensor_tensor(out, whole, high_.bitcast(F32), ALU.subtract)

            dve.sem_inc(mul_done, 1)
            dve.sem_inc(act_split, 1)
            dve.sem_inc(out_made, 1)

            dve.memset(scales_raw[:, SC_STAT[0]:SC_ALL], 0.0).then_inc(s_zero, 1)
            steps = [0]

            def step(ins):
                steps[0] += 1
                ins.then_inc(s_step, 1)
                dve.wait_ge(s_step, steps[0])

            def expm1(n, x):
                T, K, R, H, PW = (v[:, 0:n] for v in (e_t, e_k, e_r, e_h, e_p))
                step(dve.tensor_scalar(e_in[:, 0:n], x, -87.0, 88.0, ALU.max, ALU.min))
                x = e_in[:, 0:n]
                step(dve.tensor_scalar(T, x, LOG2E, MAGIC + 127.0, ALU.mult, ALU.add))
                step(dve.tensor_scalar(K, T, -(MAGIC + 127.0), None, ALU.add))
                step(dve.tensor_single_scalar(PW, T.bitcast(I32), 23, op=ALU.logical_shift_left))
                step(dve.scalar_tensor_tensor(R, K, -LN2_HI, x, ALU.mult, ALU.add))
                step(dve.scalar_tensor_tensor(R, K, -LN2_LO, R, ALU.mult, ALU.add))
                step(dve.tensor_scalar(H, R, 1.0 / 5040, None, ALU.mult))
                for c in (1.0 / 720, 1.0 / 120, 1.0 / 24, 1.0 / 6, 0.5, 1.0):
                    step(dve.scalar_tensor_tensor(H, H, c, R, ALU.add, ALU.mult))

            dve.wait_ge(s_par, 48)
            expm1(2, pack[:, 0:2, :])
            pw = e_p[:].bitcast(F32)
            step(dve.tensor_tensor(e_out[:], pw, e_h[:], ALU.mult))
            step(dve.tensor_tensor(e_out[:], e_out[:], pw, ALU.add))
            ea, dt, ai = e_out[:, 0, :], e_out[:, 1, :], pack[:, 2, :]
            dve.scalar_tensor_tensor(rho[:], ea, -1.0, dt, ALU.mult, ALU.mult)
            step(dve.tensor_tensor(theta[:], ai, dt, ALU.mult))
            dve.tensor_scalar(turns[:], theta[:], 1 / (2 * math.pi), None, ALU.mult)
            step(dve.tensor_scalar(theta_h[:], theta[:], 1 / (2 * math.pi), None, ALU.mult))
            high_turns = theta_h[:].bitcast(F32)
            step(dve.scalar_tensor_tensor(theta_l[:], high_turns, -TWO_PI_1, theta[:], ALU.mult, ALU.add))
            step(dve.scalar_tensor_tensor(theta_l[:], high_turns, -TWO_PI_2, theta_l[:], ALU.mult, ALU.add))
            step(dve.tensor_scalar(theta_l[:], theta_l[:], 1 / (2 * math.pi), None, ALU.mult))
            dve.sem_inc(s_th, 1)
            for q in range(SEQ // HQ):
                hs = slice(q * HQ, (q + 1) * HQ)
                T, H, L = ph_t[:, hs], ph_h[:, hs], ph_l[:, hs]
                groups = ((PH_S, PH_C, 0.0, -HALF_TURN, HALF_TURN),
                          (PH_C, PH_Q, 0.25, -HALF_TURN - 0.25, HALF_TURN - 0.25),
                          (PH_Q, NPH, offs[:, 0:1], offs[:, 1:2], offs[:, 2:3]))
                step(dve.tensor_tensor(T, turns[:, hs].unsqueeze(2).to_broadcast([P, HQ, NPH]),
                                       mult[:].unsqueeze(1).to_broadcast([P, HQ, NPH]), ALU.mult))
                for n0, n1, off, _, _ in groups:
                    last = dve.tensor_scalar(T[:, :, n0:n1], T[:, :, n0:n1], off, MAGIC, ALU.add, ALU.add)
                step(last)
                if q == 0:
                    AE, AI2 = (cw[:, n, :] for n in (5, 6))
                    dve.scalar_tensor_tensor(AE, ea, 0.5, ea, ALU.mult, ALU.mult)
                    step(dve.scalar_tensor_tensor(AI2, ai, 0.5, ai, ALU.mult, ALU.mult))
                    step(dve.tensor_tensor(AE, AE, AI2, ALU.add))
                    dve.reciprocal(INV2, AE).then_inc(s_inv, 1)
                dve.wait_ge(s_prod, 2 * q + 1)
                step(dve.scalar_tensor_tensor(T, T, -MAGIC, H, ALU.add, ALU.subtract))
                dve.wait_ge(s_prod, 2 * q + 2)
                step(dve.tensor_tensor(T, L, T, ALU.subtract))
                for n0, n1, _, least, most in groups:
                    last = dve.tensor_scalar(T[:, :, n0:n1], T[:, :, n0:n1], least, most, ALU.max, ALU.min)
                last.then_inc(s_red, 1)

            expm1(1, rho[:].unsqueeze(1))
            pw = e_p[:, 0, :].bitcast(F32)
            step(dve.tensor_tensor(em1[:], pw, e_h[:, 0, :], ALU.mult))
            step(dve.scalar_tensor_tensor(em1[:], pw, -1.0, em1[:], ALU.add, ALU.add))
            dve.wait_ge(s_sin, SEQ // HQ)
            W, ER, EI, T0, T1, T2, T3, AL, BE = (cw[:, n, :] for n in range(5, 14))
            s1, sh = trig[:, :, PH_S + LA], trig[:, :, PH_S + LA + 1]
            dve.scalar_tensor_tensor(EI, em1[:], 1.0, s1, ALU.add, ALU.mult)
            step(dve.scalar_tensor_tensor(W, sh, -2.0, sh, ALU.mult, ALU.mult))
            step(dve.scalar_tensor_tensor(ER, em1[:], 1.0, W, ALU.add, ALU.mult))
            step(dve.tensor_tensor(ER, ER, em1[:], ALU.add))
            dve.wait_ge(s_g, 1)
            dve.tensor_tensor(T0, GR, ER, ALU.mult)
            dve.tensor_tensor(T1, GI, EI, ALU.mult)
            dve.tensor_tensor(T2, GI, ER, ALU.mult)
            step(dve.tensor_tensor(T3, GR, EI, ALU.mult))
            dve.tensor_tensor(AL, T0, T1, ALU.add)
            step(dve.tensor_tensor(BE, T2, T3, ALU.subtract))
            sn, cs = trig[:, :, PH_S:PH_S + LA], trig[:, :, PH_C:PH_C + LA]
            dve.tensor_tensor(sn, sn, BE.unsqueeze(2).to_broadcast([P, SEQ, LA]), ALU.mult)
            step(dve.tensor_tensor(pfac[:], cs, AL.unsqueeze(2).to_broadcast([P, SEQ, LA]), ALU.mult))
            step(dve.tensor_tensor(pfac[:], pfac[:], sn, ALU.add))
            dve.wait_ge(s_dec, 1)
            dve.tensor_tensor(pfac[:], pfac[:], decay[:, :, 0:LA], ALU.mult).then_inc(s_fac, 1)

            dve.wait_ge(s_cst, 16 * 8)
            dve.tensor_copy(len_rowf[:], len_row[:])
            step(dve.tensor_copy(len_f[:], len_i[:]))
            for j in range(KD):
                last = dve.tensor_scalar(mask_t[:, j, :], len_rowf[:], place[:, j:j + 1], None, ALU.is_gt)
            last.then_inc(s_mask, 1)
            dve.tensor_scalar(mask[:], mask[:], len_f[:, 0:1], None, ALU.is_lt).then_inc(s_mask, 1)
            dve.tensor_scalar(nbthr[:, 1:2], nbthr[:, 0:1], -1.0, None, ALU.mult).then_inc(s_mask, 1)
            for j in range(2):
                dve.wait_ge(s_kh, j + 1)
                hs = slice(j * SEQ // 2, (j + 1) * SEQ // 2)
                low(k_r[:, 1, hs, :], ps_k[j][0:LA, :].rearrange("a (h c) -> a h c", c=LC), k_r[:, 0, hs, :]
                    ).then_inc(s_ks, 1)

            def u_low(i, off):
                h, slot, k = position(i, off)
                if exists(h):
                    dve.wait_ge(ut_hi, h + 1)
                    low(ut_r[:, slot, 1], um[:, slot], ut_r[:, slot, 0]).then_inc(ut_done, 1)

            u_low(0, 0)
            u_low(0, 1)

            dve.wait_ge(s_whi, 1)
            low(base_r[:, 1], wstage[:], base_r[:, 0]).then_inc(s_wsp, 1)
            dve.wait_ge(s_whi, 2)
            low(ag_r[:, :, 1], ag_raw[:], ag_r[:, :, 0])
            low(moeb_r[:, 1], moeb_raw[:], moeb_r[:, 0]).then_inc(s_wsp, 1)

            dve.wait_ge(s_b1, 64)
            dve.tensor_copy(idx_f[:], idx_i[:]).then_inc(idx_step, 1)
            dve.wait_ge(idx_step, 1)
            dve.tensor_scalar(idx_f[:], idx_f[:], 0.0, float(ADAPTERS - 1), ALU.max, ALU.min).then_inc(idx_step, 1)
            dve.wait_ge(idx_step, 2)
            dve.tensor_scalar(idx_f[:], idx_f[:], float(RANK1), rowid[:, 0:1], ALU.mult, ALU.add
                              ).then_inc(idx_step, 1)
            dve.wait_ge(idx_step, 3)
            dve.tensor_copy(idx_u[:], idx_f[:]).then_inc(idx_ready, 1)

            def apply_scales(tile, banks=ps_w):
                n, m, a, q = tile
                _, _, w, width = tile_ops(m, a, q)
                dve.wait_ge(s_big[m], 16 if m == 1 else 64)
                dve.wait_ge(s_wfull, n + 1)
                dve.tensor_tensor(w, w, banks[a % 2][:, 0:width], ALU.mult).then_inc(s_wmul, 1)

            GS = 9

            def turn(i, off, tiles):
                h, slot, k = position(i, off)
                p, pslot, pk = position(i, off - 1)
                if exists(p):
                    dve.wait_ge(hwt_hi, p + 1)
                    low(hwt_r[:, pslot, 1], ps_th[:, 0:P], hwt_r[:, pslot, 0]).then_inc(hwt_done, 1)
                if exists(h):
                    sm = small[:, slot]
                    e0 = EXPERTS * RANK0
                    done = [0]

                    def gstep(ins):
                        done[0] += 1
                        ins.then_inc(g_step, 1)
                        dve.wait_ge(g_step, GS * h + done[0])

                    dve.wait_ge(ag_copied, h + 1)
                    gstep(dve.tensor_tensor(ag_sum[:], ag_sum[:], ps_s[:, 0:AGW], ALU.add))
                    gstep(dve.tensor_reduce(sm[:, 0:1], ag_sum[:, e0:e0 + EXPERTS], AX.X, ALU.max))
                    dve.tensor_scalar(sm[:, 8:16], ag_sum[:, e0:e0 + EXPERTS], sm[:, 0:1], None, ALU.subtract
                                      ).then_inc(sh_done, 1)
                if not (isinstance(i, int) and 2 * i + off + 3 < 2):
                    u_low(i, off + 3)
                if exists(h):
                    dve.wait_ge(ex_done, h + 1)
                    gstep(dve.tensor_scalar(sm[:, 2:3], sm[:, 2:3], 1.0, 8.0, ALU.add, ALU.mult))
                    gstep(dve.reciprocal(sm[:, 3:5], sm[:, 1:3]))
                    gstep(dve.tensor_scalar(sm[:, 24:32], sm[:, 16:24], sm[:, 3:4], sm[:, 4:5],
                                            ALU.mult, ALU.subtract))
                    gstep(dve.tensor_scalar(sm[:, 24:32], sm[:, 24:32], 0.0, None, ALU.max))
                    gstep(dve.tensor_reduce(sm[:, 5:6], sm[:, 24:32], AX.X, ALU.add))
                    gstep(dve.scalar_tensor_tensor(sm[:, 5:6], sm[:, 5:6], 0.0, sm[:, 5:6],
                                                   ALU.is_equal, ALU.add))
                    gstep(dve.reciprocal(sm[:, 6:7], sm[:, 5:6]))
                    assert done[0] == GS
                    dve.tensor_scalar(sm[:, 32:40], sm[:, 24:32], sm[:, 6:7], 2.0, ALU.mult, ALU.mult
                                      ).then_inc(w_done, 1)
                    dve.wait_ge(w_done, h + 1)
                    dve.tensor_tensor(hw[:].rearrange("p (e r) -> p e r", r=RANK0),
                                      ag_sum[:, 0:e0].rearrange("p (e r) -> p e r", r=RANK0),
                                      sm[:, 32:40].unsqueeze(2).to_broadcast([P, EXPERTS, RANK0]), ALU.mult
                                      ).then_inc(hw_done, 1)
                n, nslot, _ = position(i, off + 1)
                if exists(n):
                    dve.wait_ge(yt_hi, n + 1)
                    low(yt_r[:, nslot, 1], ps_ty[:], yt_r[:, nslot, 0]).then_inc(yt_done, 1)
                if exists(p):
                    dve.wait_ge(moe_done, p + 1)
                    dve.wait_ge(xb_done, p + 1)
                    wait(dve, x1_out[pslot], 16 * pk)
                    dve.tensor_tensor(x1t[:, pslot, :], ps_b[pslot][:], xr[:, pslot, :], ALU.add
                                      ).then_inc(x1_done, 1)
                if tiles:
                    apply_scales(tiles[0])
                if tiles:
                    apply_scales(tiles[1])
                v, vslot, _ = position(i, off + 2)
                if exists(v):
                    dve.wait_ge(conv_done, v + 1)
                    wait(dve, ty_done, v)
                    dve.tensor_tensor(ym[:], ps_y[:], mask[:], ALU.mult).then_inc(ym_done, 1)

            phase_a(dve, turn)
            for c in range(2 * DOWN_TURNS, CH):
                apply_scales(down_tile(c), free_banks)


            def split_gu(c, n):
                c, slot, _ = at_chunk(c)
                dve.wait_ge(gate_hi, n + 1)
                low(gate_r[slot][:, 1], gate_w[:, :, bass.ds(c * P, P)], gate_r[slot][:, 0]).then_inc(gate_split, 1)
                dve.wait_ge(up_hi, n + 1)
                low(up_r[slot][:, 1], up_w[:, :, bass.ds(c * P, P)], up_r[slot][:, 0]).then_inc(up_split, 1)

            def unit_in(g, u):
                s = 2 * g + u
                for j in unit_order(g, u):
                    if j == 2:
                        dve.wait_ge(at_hi, s + 1)
                        low(at_r[:, 1], bank[2][:].rearrange("p (k n) -> p k n", k=KD), at_r[:, 0]
                            ).then_inc(at_split, 1)
                    else:
                        dve.wait_ge(xt_hi, 2 * s + j + 1)
                        low(xt_r[u][:, 1, 2 * j:2 * j + 2, :], bank[j][:].rearrange("p (k n) -> p k n", k=2),
                            xt_r[u][:, 0, 2 * j:2 * j + 2, :]).then_inc(xt_split, 1)

            def unit_b(g, u):
                for j, cols in enumerate(B_HALVES):
                    dve.wait_ge(bg_hi, 4 * g + 2 * u + j + 1)
                    low(bg_r[:, 1, cols], b_raw[:, cols], bg_r[:, 0, cols]).then_inc(bg_split, 1)

            def unit_h(g, u):
                b, n = H_BANK[u]
                dve.wait_ge(full[b], 10 * g + n + 1)
                dve.tensor_tensor(hm[:], bank[b][:, 0:UT], blockmask[:], ALU.mult).then_inc(hm_made, 1)
                dve.wait_ge(hm_hi, 2 * g + u + 1)
                low(hm_r[:, u, 1], hm[:], hm_r[:, u, 0]).then_inc(hm_split, 1)

            def unit_z(g, u, j):
                b, n = Z_BANK[u][j]
                dve.wait_ge(z_hi, 4 * g + 2 * u + j + 1)
                for o in range(2):
                    k = 2 * j + o
                    last = dve.scalar_tensor_tensor(z_r[:, 1, k, u * UT:(u + 1) * UT],
                                                    bank[b][:, o * UT:(o + 1) * UT], bias1[:, k:k + 1],
                                                    z_r[:, 0, k, u * UT:(u + 1) * UT].bitcast(F32),
                                                    ALU.add, ALU.subtract)
                last.then_inc(z_split, 1)

            def chunk(g, c, nxt, mid=None):
                cc, slot, k = at_chunk(c)
                n = CH * g + cc
                dve.wait_ge(down_hi, n + 1)
                low(down_r[slot][:, 1], down_w[:, bass.ds(cc, 1), :].rearrange("p a d -> p (a d)"),
                    down_r[slot][:, 0]).then_inc(down_split, 1)
                dve.wait_ge(silu_done, n + 1)
                dve.wait_ge(full[2 * slot + 1], 10 * g + 4 + k)
                dve.wait_ge(act_split, n + 1)
                dve.tensor_tensor(act32[:], silu[:], bank[2 * slot + 1][:], ALU.mult).then_inc(mul_done, 1)
                if mid:
                    mid()
                dve.wait_ge(act_hi, n + 1)
                low(act_r[slot][:, 1], act32[:], act_r[slot][:, 0]).then_inc(act_split, 1)
                if nxt is not None:
                    split_gu(nxt, n + 2)

            def evacuate_last():
                dve.wait_ge(res_in, 16 * NG)
                for n in range(GT // P):
                    dve.wait_ge(tile_done, n + 1)
                    dve.tensor_tensor(res[:, n, :], acc[n][:], res[:, n, :], ALU.add).then_inc(tile_made, 1)

            def evacuate(g):
                dve.wait_ge(down_done, CH * (g + 1) + 2)
                dve.wait_ge(res_in, 16 * (g + 1))
                for n in range(GT // P):
                    last = dve.tensor_tensor(res[:, n, :], acc[n][:], res[:, n, :], ALU.add)
                last.then_inc(out_made, 1)

            def unit_rest(g, mid=None):
                unit_b(g, 0)
                unit_h(g, 0)
                unit_in(g, 1)
                if mid:
                    mid()
                unit_z(g, 0, 0)
                unit_h(g, 1)
                unit_b(g, 1)
                unit_z(g, 0, 1)
                unit_z(g, 1, 0)
                unit_z(g, 1, 1)

            def group(g, last):
                with dve.Fori(0, CH // 2 - 1) as i:
                    chunk(g, pair(i, 0), pair(i, 2))
                    chunk(g, pair(i, 1), pair(i, 3))
                if last:
                    chunk(g, CH - 2, None)
                    chunk(g, CH - 1, None)
                    evacuate_last()
                    return
                chunk(g, CH - 2, 0)
                chunk(g, CH - 1, 1, mid=lambda: unit_in(g + 1, 0))
                unit_rest(g + 1)
                evacuate(g)

            unit_in(0, 0)
            dve.wait_ge(proj_hi, 1)
            low(proj_r[:, 1], wstage[:], proj_r[:, 0]).then_inc(proj_split, 1)
            unit_rest(0, lambda: (split_gu(0, 0), split_gu(1, 1)))
            with dve.Fori(0, NG - 1) as g:
                group(g, False)
            group(NG - 1, True)

        @block.tensor
        def _(pe):
            pe.sem_inc(down_done, 2)
            pe.sem_inc(s_wmul, 2)

            def split3(out, w, x, start=True, stop=True):
                n, total = 0, len(w) * len(PASSES)
                for wk, xk in zip(w, x):
                    for a, b in PASSES:
                        last = pe.matmul(out, wk[a], xk[b], start=start and n == 0, stop=stop and n == total - 1)
                        n += 1
                return last

            def keep_busy(bank_, n):
                for _ in range(n):
                    pe.transpose(bank_[:, 0:P], ident[:], ident[:])

            pe.wait_ge(s_cst, 16 * 8)
            pe.wait_ge(s_sin, SEQ // HQ)
            keep_busy(ps_w[0], 26)
            pe.wait_ge(s_fac, 2)
            for j in range(2):
                pe.matmul(ps_k[j][0:LA, :], ident[0:1, 0:LA], dpad[:, j * DIM:(j + 1) * DIM], start=True, stop=False)
                for hh in range(SEQ // 2):
                    h = j * SEQ // 2 + hh
                    last = pe.matmul(ps_k[j][0:LA, hh * LC:(hh + 1) * LC], pfac[:, h, :], decay[:, h, LA:NDEC],
                                     start=False, stop=hh == SEQ // 2 - 1)
                last.then_inc(s_k, 1)

            def scale_tile(tile, banks=ps_w):
                n, m, a, q = tile
                lhs, rhs, _, width = tile_ops(m, a, q)
                pe.wait_ge(s_tsp, (6, 3, 9)[m])
                pe.wait_ge(s_wmul, n + 1)
                pe.matmul(banks[a % 2][:, 0:width], lhs, rhs, start=True, stop=True).then_inc(s_wfull, 1)

            keep_busy(ps_w[0], 52)

            def turn(i, off, tiles):
                h, slot, k = position(i, off)
                p, pslot, _ = position(i, off - 1)
                n, nslot, _ = position(i, off + 1)
                v, vslot, vk = position(i, off + 2)
                yt = [[yt_r[:, slot, part, j, :] for part in range(2)] for j in range(KD)]
                if exists(h):
                    if isinstance(h, int) and h == 0:
                        pe.wait_ge(s_wsp, 2)
                    pe.wait_ge(yt_done, h + 1)
                    wait(pe, hw_done, h)
                    for j in range(KD):
                        pe.matmul(ps_s[:, 0:2 * AGW], yt[j][0], ag_r[:, j].rearrange("p s n -> p (s n)"),
                                  start=j == 0, stop=False)
                        last = pe.matmul(ps_s[:, 0:AGW], yt[j][1], ag_r[:, j, 0], start=False, stop=j == KD - 1)
                    last.then_inc(ag_done, 1)
                    wait(pe, x1_done, h - 1)
                    base = [[base_r[:, part, j, :] for part in range(2)] for j in range(KD)]
                    split3(ps_b[slot][:], yt[0:2], base[0:2], stop=False)
                if exists(p):
                    pe.wait_ge(hwt_done, p + 1)
                    split3(ps_b[pslot][:], [[hwt_r[:, pslot, part, :] for part in range(2)]],
                           [[moeb_r[:, part, :] for part in range(2)]], start=False).then_inc(moe_done, 1)
                if tiles:
                    scale_tile(tiles[0])
                if exists(n):
                    pe.wait_ge(ym_done, n + 1)
                    wait(pe, yt_done, n)
                    for j in range(KD):
                        last = pe.transpose(ps_ty[:, j, :], ym[:, j * P:(j + 1) * P], ident[:])
                    last.then_inc(ty_done, 1)
                if exists(h):
                    split3(ps_b[slot][:], yt[2:4], base[2:4], start=False, stop=False).then_inc(base_done, 1)
                if tiles:
                    scale_tile(tiles[1])
                if exists(v):
                    pe.wait_ge(ut_done, v + 1)
                    pe.wait_ge(toep_in[vslot], 16 * (vk + 1))
                    wait(pe, ym_done, v)
                    for j in range(KD):
                        last = split3(ps_y[:, j * P:DIM], [[ut_r[:, vslot, part, j, :] for part in range(2)]],
                                      [[toep[:, vslot, part, 0:DIM - j * P] for part in range(2)]],
                                      start=j == 0, stop=j == KD - 1)
                    last.then_inc(conv_done, 1)
                if exists(h):
                    pe.wait_ge(hw_done, h + 1)
                    wait(pe, hwt_done, h)
                    pe.transpose(ps_th[:, 0:P], hw[:], ident[:]).then_inc(thw_done, 1)

            phase_a(pe, turn)
            for c in range(2 * DOWN_TURNS, CH):
                scale_tile(down_tile(c), free_banks)
                keep_busy(ps_th, 3)

            def unit_in(g, u):
                s = 2 * g + u
                for j in unit_order(g, u):
                    if j == 2:
                        pe.wait_ge(a_in, 16 * (s + 1))
                        if u:
                            pe.wait_ge(at_split, 2 * g + 1)
                        else:
                            wait(pe, silu_done, CH * g)
                        for k in range(KD):
                            last = pe.transpose(bank[2][:, k * P:(k + 1) * P], a_raw[:, k * P:(k + 1) * P], ident[:])
                        last.then_inc(full[2], 1)
                        continue
                    if j == 0:
                        if isinstance(s, int) and s == 0:
                            pe.wait_ge(xt_first, 16 * (P // SEQ + 4))
                        else:
                            pe.wait_ge(xt_in, 16 * s)
                    if u:
                        pe.wait_ge(xt_split, 4 * g + 1 + j)
                    elif j == 0:
                        wait(pe, silu_done, CH * g - 1)
                    else:
                        wait(pe, mul_done, CH * g)
                    for kk in range(2):
                        k = 2 * j + kk
                        for tt in range(2):
                            last = pe.transpose(bank[j][:, kk * UT + tt * P:kk * UT + (tt + 1) * P],
                                                xt[:, tt, k * P:(k + 1) * P], ident[:])
                    last.then_inc(full[j], 1)

            def unit_h(g, u):
                b, _ = H_BANK[u]
                pe.wait_ge(at_split, 2 * g + u + 1)
                if not u:
                    wait(pe, mul_done, CH * g + 1)
                for j in range(2):
                    pe.wait_ge(xt_split, 4 * g + 2 * u + 1 + j)
                    ks = (2 * j, 2 * j + 1)
                    last = split3(bank[b][:, 0:UT], [[at_r[:, part, k, :] for part in range(2)] for k in ks],
                                  [[xt_r[u][:, part, k, :] for part in range(2)] for k in ks],
                                  start=j == 0, stop=j == 1)
                last.then_inc(full[b], 1)

            def unit_z(g, u, j):
                b, _ = Z_BANK[u][j]
                if (u, j) == (0, 0):
                    pe.wait_ge(hm_made, 2 * g + 1)
                elif (u, j) == (0, 1):
                    pe.wait_ge(xt_split, 4 * g + 3)
                elif (u, j) == (1, 0):
                    pe.wait_ge(at_split, 2 * g + 2)
                else:
                    pe.wait_ge(z_split, 4 * g + 1)
                for o in range(2):
                    c = 2 * j + o
                    out = bank[b][:, o * UT:(o + 1) * UT]
                    split3(out, [[proj_r[:, part, k, c * P:(c + 1) * P] for part in range(2)] for k in range(KD)],
                           [[xt_r[u][:, part, k, :] for part in range(2)] for k in range(KD)], stop=False)
                    if o == 0:
                        pe.wait_ge(hm_split, 2 * g + u + 1)
                        pe.wait_ge(bg_split, 4 * g + 2 * u + j + 1)
                    last = split3(out, [[bg_r[:, part, c * P:(c + 1) * P] for part in range(2)]],
                                  [[hm_r[:, u, part, :] for part in range(2)]], start=False)
                last.then_inc(full[b], 1)

            def gate_up(g, c):
                cc, slot, _ = at_chunk(c)
                n = CH * g + cc
                z = [[z_r[:, part, k, :] for part in range(2)] for k in range(KD)]
                for w, split, b, before in ((gate_r, gate_split, 2 * slot, silu_done),
                                            (up_r, up_split, 2 * slot + 1, mul_done)):
                    pe.wait_ge(split, n + 1)
                    if isinstance(c, int) and c == 0 and w is gate_r:
                        pe.wait_ge(z_split, 4 * g + 3)
                        ws = [[w[slot][:, part, k, :] for part in range(2)] for k in range(KD)]
                        split3(bank[b][:], ws[0:2], z[0:2], stop=False)
                        pe.wait_ge(z_split, 4 * g + 4)
                        split3(bank[b][:], ws[2:4], z[2:4], start=False).then_inc(full[b], 1)
                        continue
                    if isinstance(c, int) and c < 2:
                        pe.wait_ge(z_split, 4 * g + 4)
                        pe.wait_ge(hm_made, 2 * g + 2)
                    else:
                        pe.wait_ge(before, n - 1 if before is silu_done else n)
                    last = split3(bank[b][:], [[w[slot][:, part, k, :] for part in range(2)] for k in range(KD)], z)
                    last.then_inc(full[b], 1)

            def down(g, c, final=False):
                cc, slot, _ = at_chunk(c)
                n = CH * g + cc
                pe.wait_ge(down_split, n + 1)
                pe.wait_ge(act_split, n + 2)
                if isinstance(c, int) and c == 0:
                    pe.wait_ge(out_made, g + 1)
                for tt in range(GT // P):
                    last = split3(acc[tt][:], [[act_r[slot][:, part, tt * P:(tt + 1) * P] for part in range(2)]],
                                  [[down_r[slot][:, part, :] for part in range(2)]],
                                  start=isinstance(c, int) and c == 0, stop=isinstance(c, int) and c == CH - 1)
                    if final:
                        last.then_inc(tile_done, 1)
                if not final:
                    last.then_inc(down_done, 1)

            def group(g, last):
                gate_up(g, 0)
                gate_up(g, 1)
                down(g, 0)
                gate_up(g, 2)
                down(g, 1)
                with pe.Fori(1, CH // 2 - 1) as i:
                    gate_up(g, pair(i, 1))
                    down(g, pair(i, 0))
                    gate_up(g, pair(i, 2))
                    down(g, pair(i, 1))
                gate_up(g, CH - 1)
                if last:
                    down(g, CH - 2)
                    down(g, CH - 1, final=True)
                    return
                unit_in(g + 1, 0)
                down(g, CH - 2)
                unit_rest(g + 1)
                down(g, CH - 1)

            def unit_rest(g):
                unit_h(g, 0)
                unit_in(g, 1)
                if isinstance(g, int) and g == 0:
                    pe.wait_ge(proj_split, 1)
                unit_z(g, 0, 0)
                unit_h(g, 1)
                unit_z(g, 0, 1)
                unit_z(g, 1, 0)
                unit_z(g, 1, 1)

            unit_in(0, 0)
            unit_rest(0)
            with pe.Fori(0, NG - 1) as g:
                group(g, False)
            group(NG - 1, True)


def kernel(**inputs):
    import numpy as np
    import concourse.bacc as bacc
    from concourse.bass_utils import run_bass_kernel_spmd

    a = {k: np.asarray(v) for k, v in inputs.items()}

    def con(v):
        return np.ascontiguousarray(v)

    def both(v):
        return np.concatenate([v.T, v.T], axis=0)

    f = np.float32
    cr, ci = a["L0_cond_C"][..., 0].T, a["L0_cond_C"][..., 1].T
    sign = np.concatenate([np.ones((NSTATE, SEQ), f), -np.ones((NSTATE, SEQ), f)])
    pack = np.stack([
        both(a["L0_cond_log_A_real"]),
        np.broadcast_to(a["L0_cond_log_dt"][None, :], (P, SEQ)),
        both(a["L0_cond_A_imag"]),
        np.concatenate([cr, ci]),
        np.concatenate([ci, cr]),
        sign], axis=1)
    la, lc = [LC * n for n in range(LA)], list(range(LC))
    table = np.broadcast_to(np.array(la + [1, 0.5] + la + lc, f), (P, NPH))
    quarter = np.where(np.arange(P) < NSTATE, 0.25, 0.0)
    offsets = np.stack([quarter, -HALF_TURN - quarter, HALF_TURN - quarter, 2 * math.pi * quarter,
                        np.full(P, math.pi / 2)], axis=1).astype(f)
    rows = np.arange(P) // RANK1
    data = {
        "x": a["x"],
        "s4_pack": con(pack),
        "phase_table": con(table),
        "phase_offsets": offsets,
        "d_row": con(np.concatenate([a["L0_cond_D"][:, None], np.zeros((SEQ, LC - 1), f)], axis=1)).reshape(1, -1),
        "ident": np.eye(P, dtype=f),
        "iota": np.arange(DIM, dtype=f),
        "lengths": con(a["itok_B_8_3872"][:, None]),
        "b_thr": a["L0_ffn_b_thr"],
        "b_base": a["L0_ffn_b_base"],
        "base_wt": con(a["L0_ffn_W_base"].T),
        "ag_wt": con(np.concatenate([a["L0_ffn_A_w"].reshape(EXPERTS * RANK0, DIM).T, a["L0_ffn_W_gate"].T,
                                     a["L0_ffn_W_thr"][:, None], np.zeros((DIM, 1), f)], axis=1)),
        "moe_bt": con(a["L0_ffn_B_w"].transpose(0, 2, 1).reshape(EXPERTS * RANK0, DIM)),
        "up_wt": con(a["L1_ffn_up_w"].T),
        "gate_wt": con(a["L1_ffn_gate_w"].T),
        "down_wt": con(a["L1_ffn_down_w"].T),
        "proj_wt": con(a["L1_cond_base_weight"].T),
        "bias1_cols": con(a["L1_cond_base_bias"].reshape(KD, P).T),
        "lora_a": con(a["L1_cond_lora_A_w"].reshape(ADAPTERS * RANK1, DIM)),
        "lora_b": con(a["L1_cond_lora_B_w"].transpose(0, 2, 1).reshape(ADAPTERS * RANK1, DIM)),
        "blockmask": con((np.arange(UT)[None, :] // SEQ == rows[:, None]).astype(f)),
        "adapter_rows": con(np.repeat(a["itok_B_6_15"].reshape(2 * NG, P // RANK1), RANK1, axis=1).T),
        "rank_rows": (np.arange(P) % RANK1).astype(f)[:, None],
        "scales": con(np.concatenate([
            a["L1_ffn_gate_su"].T, a["L1_ffn_up_su"].T, a["L1_ffn_down_su"].T,
            a["L1_ffn_gate_sv"], a["L1_ffn_up_sv"], a["L1_ffn_down_sv"]], axis=1)),
        "x_t": con(a["x"].transpose(1, 2, 0).reshape(SEQ, KD, P, BATCH)[:, :, ::-1, :].transpose(0, 2, 1, 3)
                   ).reshape(SEQ, P, KD * BATCH),
        "lengths_row": con(a["itok_B_8_3872"]),
        "place": con((np.arange(KD)[None, :] * P + (P - 1 - np.arange(P))[:, None]).astype(f)),
    }
    nc = bacc.Bacc("TRN2", target_bir_lowering=False, num_devices=1)
    t, arrays = {}, {}
    for name, v in data.items():
        v = np.ascontiguousarray(v)
        arrays[f"in_{name}"] = v
        t[name] = nc.dram_tensor(f"in_{name}", v.shape, mybir.dt.from_np(v.dtype), kind="ExternalInput").ap()
    t["out"] = nc.dram_tensor("out_x", (BATCH, SEQ, DIM), F32, kind="ExternalOutput").ap()
    build(nc, t)
    r = run_bass_kernel_spmd(nc, [arrays], core_ids=[0])
    return r.results[0]["out_x"]
```
